# Optimizing a Trainium2 kernel written in Bass

```python
import numpy as np
import jax
import jax.numpy as jnp

def _softmax(x, axis=-1):
    return jax.nn.softmax(x, axis=axis)

def _gelu(x):
    return jax.nn.gelu(x, approximate=True)

def _silu(x):
    return jax.nn.silu(x)

def _sigmoid(x):
    return jax.nn.sigmoid(x)

def _layernorm(x, axis=-1, eps=1e-05):
    m = jnp.mean(x, axis=axis, keepdims=True)
    v = jnp.var(x, axis=axis, keepdims=True)
    return (x - m) / jnp.sqrt(v + eps)

def _scatter_add(tgt, idx, src, axis=0):
    return tgt.at[idx].add(src)

def _segment_sum(src, seg, n):
    return jax.ops.segment_sum(src, seg, n)
kernel_name = 'mk_vit_tower_d1_tok_img256_r4_34f72c'

def setup_inputs(seed: int=0):
    np.random.seed(seed)
    _w = jnp.asarray

    def _rec_inputs():
        import jax
        import jax.numpy as jnp
        _rk = jax.random.key(seed)
        x = -0.000392918 + 0.999932 * jax.random.normal(jax.random.fold_in(_rk, 1), (16, 1, 128, 512), jnp.float32)
        return x
    x = _rec_inputs()

    def _L0_tok_setup():
        import jax, jax.numpy as jnp
        import numpy as np
        PATCH = 8
        EMBED = 64
        N_MELS = 128
        N_FRAMES = 512
        BATCH = 64
        NUM_PATCHES = N_MELS // PATCH * (N_FRAMES // PATCH)
        key = jax.random.key(seed)
        k1, k2, k3, k4 = jax.random.split(key, 4)
        x = jax.random.normal(k1, (BATCH, 1, N_MELS, N_FRAMES), dtype=jnp.float32)
        W = jax.random.normal(k2, (EMBED, PATCH * PATCH), dtype=jnp.float32) * (1.0 / np.sqrt(PATCH * PATCH))
        b = jax.random.normal(k3, (EMBED,), dtype=jnp.float32) * 0.01
        pos_embed = jax.random.normal(k4, (1, NUM_PATCHES, EMBED), dtype=jnp.float32) * 0.02
        return {'x': x, 'W': W, 'b': b, 'pos_embed': pos_embed}
    _L0_tok_all = _L0_tok_setup()
    _L0_tok_in = {k: v for k, v in _L0_tok_all.items() if k in ('W', 'b', 'pos_embed')}
    del _L0_tok_all

    def _L0_attn_setup():
        import jax, jax.numpy as jnp
        import numpy as np
        IN_C = 64
        KEY_C = 64
        VAL_C = 64
        HEADS = 8
        key = jax.random.key(seed)
        ks = jax.random.split(key, 9)
        s = 0.02
        return {'x': jax.random.normal(ks[0], (4, 2048, IN_C), dtype=jnp.float32), 'Wk': jax.random.normal(ks[1], (KEY_C, IN_C), dtype=jnp.float32) * s, 'bk': jax.random.normal(ks[2], (KEY_C,), dtype=jnp.float32) * s, 'Wq': jax.random.normal(ks[3], (KEY_C, IN_C), dtype=jnp.float32) * s, 'bq': jax.random.normal(ks[4], (KEY_C,), dtype=jnp.float32) * s, 'Wv': jax.random.normal(ks[5], (VAL_C, IN_C), dtype=jnp.float32) * s, 'bv': jax.random.normal(ks[6], (VAL_C,), dtype=jnp.float32) * s, 'Wr': jax.random.normal(ks[7], (IN_C, VAL_C), dtype=jnp.float32) * s, 'br': jax.random.normal(ks[8], (IN_C,), dtype=jnp.float32) * s}
    _L0_attn_all = _L0_attn_setup()
    _L0_attn_in = {k: v for k, v in _L0_attn_all.items() if k in ('Wk', 'bk', 'Wq', 'bq', 'Wv', 'bv', 'Wr', 'br')}
    del _L0_attn_all

    def _L0_ffn_setup():
        import jax, jax.numpy as jnp
        import numpy as np
        D_MODEL = 64
        N_EXPERTS = 16
        HIDDEN = 128
        SCALE = 0.02
        key = jax.random.key(seed)
        ks = jax.random.split(key, 5)
        x = jax.random.normal(ks[0], (4, 2048, D_MODEL), dtype=jnp.float32)
        gate_w = jax.random.normal(ks[1], (D_MODEL, N_EXPERTS), dtype=jnp.float32) * SCALE
        gate_b = jnp.zeros((N_EXPERTS,), dtype=jnp.float32)
        w1 = jax.random.normal(ks[2], (N_EXPERTS, D_MODEL, HIDDEN), dtype=jnp.float32) * SCALE
        w2 = jax.random.normal(ks[3], (N_EXPERTS, D_MODEL, HIDDEN), dtype=jnp.float32) * SCALE
        w3 = jax.random.normal(ks[4], (N_EXPERTS, HIDDEN, D_MODEL), dtype=jnp.float32) * SCALE
        return {'x': x, 'gate_w': gate_w, 'gate_b': gate_b, 'w1': w1, 'w2': w2, 'w3': w3}
    _L0_ffn_all = _L0_ffn_setup()
    _L0_ffn_in = {k: v for k, v in _L0_ffn_all.items() if k in ('gate_w', 'gate_b', 'w1', 'w2', 'w3')}
    del _L0_ffn_all
    return {'x': x, 'L0_tok_W': _L0_tok_in['W'], 'L0_tok_b': _L0_tok_in['b'], 'L0_tok_pos_embed': _L0_tok_in['pos_embed'], 'L0_attn_Wk': _L0_attn_in['Wk'], 'L0_attn_bk': _L0_attn_in['bk'], 'L0_attn_Wq': _L0_attn_in['Wq'], 'L0_attn_bq': _L0_attn_in['bq'], 'L0_attn_Wv': _L0_attn_in['Wv'], 'L0_attn_bv': _L0_attn_in['bv'], 'L0_attn_Wr': _L0_attn_in['Wr'], 'L0_attn_br': _L0_attn_in['br'], 'L0_ffn_gate_w': _L0_ffn_in['gate_w'], 'L0_ffn_gate_b': _L0_ffn_in['gate_b'], 'L0_ffn_w1': _L0_ffn_in['w1'], 'L0_ffn_w2': _L0_ffn_in['w2'], 'L0_ffn_w3': _L0_ffn_in['w3']}

def reference(x, L0_tok_W, L0_tok_b, L0_tok_pos_embed, L0_attn_Wk, L0_attn_bk, L0_attn_Wq, L0_attn_bq, L0_attn_Wv, L0_attn_bv, L0_attn_Wr, L0_attn_br, L0_ffn_gate_w, L0_ffn_gate_b, L0_ffn_w1, L0_ffn_w2, L0_ffn_w3):
    import jax
    import jax.numpy as jnp

    def _L0_tok_ref(x, W, b, pos_embed):
        import jax, jax.numpy as jnp
        import numpy as np
        PATCH = 8
        EMBED = 64
        N_MELS = 128
        N_FRAMES = 512
        BATCH = 64
        NUM_PATCHES = N_MELS // PATCH * (N_FRAMES // PATCH)
        B = x.shape[0]
        mp, fp = (N_MELS // PATCH, N_FRAMES // PATCH)
        xs = x[:, 0]
        patches = xs.reshape(B, mp, PATCH, fp, PATCH).transpose(0, 1, 3, 2, 4).reshape(B, mp * fp, PATCH * PATCH)
        emb = jnp.einsum('bnk,ek->bne', patches, W) + b
        return emb + pos_embed

    def _L0_attn_ref(x, Wk, bk, Wq, bq, Wv, bv, Wr, br):
        import jax, jax.numpy as jnp
        import numpy as np
        IN_C = 64
        KEY_C = 64
        VAL_C = 64
        HEADS = 8
        n, N, c = x.shape
        xi = x.reshape(n, c, N)
        K = jnp.einsum('oc,ncs->nos', Wk, xi) + bk[None, :, None]
        Q = jnp.einsum('oc,ncs->nos', Wq, xi) + bq[None, :, None]
        V = jnp.einsum('oc,ncs->nos', Wv, xi) + bv[None, :, None]
        dk = KEY_C // HEADS
        dv = VAL_C // HEADS
        Kh = K.reshape(n, HEADS, dk, N)
        Qh = Q.reshape(n, HEADS, dk, N)
        Vh = V.reshape(n, HEADS, dv, N)
        Kh = jax.nn.softmax(Kh, axis=3)
        Qh = jax.nn.softmax(Qh, axis=2)
        ctx = jnp.einsum('nhks,nhvs->nhkv', Kh, Vh)
        att = jnp.einsum('nhkv,nhks->nhvs', ctx, Qh)
        agg = att.reshape(n, VAL_C, N)
        rep = jnp.einsum('ov,nvs->nos', Wr, agg) + br[None, :, None]
        out = rep + xi
        return jnp.transpose(out, (0, 2, 1))

    def _L0_ffn_ref(x, gate_w, gate_b, w1, w2, w3):
        import jax, jax.numpy as jnp
        import numpy as np
        D_MODEL = 64
        N_EXPERTS = 16
        HIDDEN = 128
        SCALE = 0.02
        n_experts = w1.shape[0]
        logits = jnp.einsum('bsd,de->bse', x, gate_w) + gate_b
        probs = jax.nn.softmax(logits, axis=-1)
        top_probs, top_idx = jax.lax.top_k(probs, 2)
        top_probs = top_probs / jnp.sum(top_probs, axis=-1, keepdims=True)
        dispatch = jnp.sum(jax.nn.one_hot(top_idx, n_experts, dtype=x.dtype) * top_probs[..., None], axis=-2)
        h1 = jnp.einsum('bsd,edh->bseh', x, w1)
        h2 = jnp.einsum('bsd,edh->bseh', x, w2)
        hidden = jax.nn.silu(h1) * h2
        expert_out = jnp.einsum('bseh,eho->bseo', hidden, w3)
        return jnp.einsum('bseo,bse->bso', expert_out, dispatch)
    h = _L0_tok_ref(x, L0_tok_W, L0_tok_b, L0_tok_pos_embed)
    h = h + _L0_attn_ref(_layernorm(h, axis=-1), L0_attn_Wk, L0_attn_bk, L0_attn_Wq, L0_attn_bq, L0_attn_Wv, L0_attn_bv, L0_attn_Wr, L0_attn_br)
    h = h + _L0_ffn_ref(_layernorm(h, axis=-1), L0_ffn_gate_w, L0_ffn_gate_b, L0_ffn_w1, L0_ffn_w2, L0_ffn_w3)
    return h

_drawn_inputs = setup_inputs


def setup_inputs(seed=0):
    import zlib

    import numpy as np

    out = dict(_drawn_inputs(seed))
    spreads = {'L0_ffn_gate_b': (0.0, 0.8)}
    factors = {'L0_tok_b': 6.007,
     'L0_tok_pos_embed': 2.849,
     'L0_attn_Wk': 8.0,
     'L0_attn_bk': 8.0,
     'L0_attn_Wq': 8.0,
     'L0_attn_bq': 8.0,
     'L0_attn_Wv': 8.0,
     'L0_attn_bv': 8.0,
     'L0_attn_Wr': 8.0,
     'L0_attn_br': 4.265,
     'L0_ffn_gate_w': 8.0,
     'L0_ffn_w1': 8.0,
     'L0_ffn_w2': 8.0,
     'L0_ffn_w3': 8.0}
    for name, (base, spread) in spreads.items():
        noise = np.random.default_rng([zlib.crc32(name.encode()), seed]).standard_normal(out[name].shape)
        drawn = base * np.exp(spread * noise) if base else spread * noise
        out[name] = jnp.asarray(drawn.astype(out[name].dtype))
    for name, factor in factors.items():
        out[name] = (out[name] * factor).astype(out[name].dtype)
    return out
```

```python
from contextlib import ExitStack

import concourse.bass as bass
from concourse import mybir

F32 = mybir.dt.float32
F32R = mybir.dt.float32r
U32 = mybir.dt.uint32
ACT = mybir.ActivationFunctionType
ALU = mybir.AluOpType
AX_X = mybir.AxisListType.X

P = 128
IMAGES, MELS, FRAMES = 16, 128, 512
PATCH = 8
E = 64
MP, FP = MELS // PATCH, FRAMES // PATCH
TOKENS = MP * FP
ROWS = TOKENS // E
HEAD = 8
EXPERTS, HIDDEN = 16, 128
EPS = 1e-5
PAIRS = IMAGES // 2
BLOCKS = TOKENS // P
CHUNK = 512
TILES = CHUNK // P
CHUNKS = 2 * TOKENS // CHUNK
SLOTS = CHUNKS * EXPERTS
EPAIRS = EXPERTS // 2
SHIFTED = FRAMES - PATCH + 1
SILUS, HIDS, GATED = 4, 4, 4
FIRST = 4

PATCHES, MEAN1, CENTER1, SQUARE1, VAR1, SCALE1 = 4, 6, 7, 9, 10, 11
QKV, MAXIMA, QCENTER, KTURN, KMAX, KSPREAD, KSUB, EXPS = 15, 24, 25, 25, 26, 27, 28, 29
CONTEXT, QSUM, QSCALE, CMASK, MIX, MSCALE, QTURN = 30, 30, 31, 31, 32, 33, 34
ATTENDED = 36
MEAN2, CENTER2, SQUARE2, VAR2, SCALE2 = 39, 40, 42, 43, 44
ROUTE = {1: 0, 2: EXPERTS, 3: 2 * EXPERTS, 0: 49}
FOLD = {0: 4, 1: 4, 2: 4, 3: 10}


def vit_kernel(nc, x, tok_w, tok_b, pos, wk, bk, wq, bq, wv, bv, wr, br, gate_w, gate_b, w1, w2, w3, out):
    gates_dram = nc.dram_tensor("gates_scratch", (2, EXPERTS, CHUNK), F32, kind="Internal").ap()
    with ExitStack() as ctx:
        def sb(name, shape, dt=F32):
            return ctx.enter_context(nc.sbuf_tensor(name, shape, dt))

        def bank(name):
            return ctx.enter_context(nc.psum_tensor(name, [P, 512], F32))

        def sem(name):
            return ctx.enter_context(nc.semaphore(name))

        ident = sb("ident", [P, P])
        fold = sb("fold", [P, E])
        ones = sb("ones", [P, P])
        head_mask = sb("head_mask", [P, P])
        tok_w_in = sb("tok_w_in", [E, 2, E])
        tok_w_perm = sb("tok_w_perm", [E, 2 * E])
        tok_wT = sb("tok_wT", [P, E])
        tok_w_both = sb("tok_w_both", [P, P])
        proj_in = sb("proj_in", [E, 4, 2, E])
        proj = sb("proj", [P, 4, P])
        qkv_bias = sb("qkv_bias", [P, 3, 2, E])
        emb_bias = sb("emb_bias", [P, E])
        out_bias = sb("out_bias", [P, E])
        pos_chan = sb("pos_chan", [P, ROWS, E])
        pos_tok = sb("pos_tok", [P, BLOCKS, E])
        gate_in = sb("gate_in", [P, EXPERTS])
        gate_hi = sb("gate_hi", [P, EXPERTS], F32R)
        gate_lo = sb("gate_lo", [P, EXPERTS], F32R)
        gate_bias = sb("gate_bias", [P, EXPERTS])
        expert_id = sb("expert_id", [P, EXPERTS])
        minus_half = sb("minus_half", [P, 2 * BLOCKS])
        w1_hi = sb("w1_hi", [P, EXPERTS, HIDDEN], F32R)
        w1_lo = sb("w1_lo", [P, EXPERTS, HIDDEN], F32R)
        w2_hi = sb("w2_hi", [P, EXPERTS, HIDDEN], F32R)
        w2_lo = sb("w2_lo", [P, EXPERTS, HIDDEN], F32R)
        w3_sb = sb("w3_sb", [P, EXPERTS, E])

        rows = sb("rows", [P, MP, FRAMES])
        hx = sb("hx", [P, TOKENS])
        squares = sb("squares", [P, TOKENS])
        stats = [[sb(f"stats{n}_{k}", [P, 2 * BLOCKS]) for k in range(5)] for n in range(2)]
        qkv = sb("qkv", [P, BLOCKS, 3 * P])
        kpart = sb("kpart", [P, P])
        kmax = sb("kmax", [P, 1])
        kdiag = sb("kdiag", [P, P])
        qmax = sb("qmax", [P, BLOCKS, 2 * E // HEAD])
        qsum = sb("qsum", [P, BLOCKS, 2 * E // HEAD])
        qinv = sb("qinv", [P, BLOCKS, 2 * E // HEAD])
        ctxT = sb("ctxT", [P, P])
        kinv = sb("kinv", [P, 1])
        mix = sb("mix", [P, P])
        qsT = sb("qsT", [P, TOKENS])
        h2 = sb("h2", [P, BLOCKS, 2, E])
        z = sb("z", [P, BLOCKS, 2, E])

        zs = [sb(f"zs{n}", [P, CHUNK], F32R) for n in range(2)]
        residual = [sb(f"residual{n}", [P, TILES, E]) for n in range(CHUNKS)]
        logits = sb("logits", [P, TILES, EXPERTS])
        top = sb("top", [P, TILES, 8])
        top_id = sb("top_id", [P, TILES, 8], U32)
        margin = sb("margin", [P, TILES])
        half_tanh = sb("half_tanh", [P, TILES])
        share = [sb(f"share{n}", [P, TILES]) for n in range(2)]
        hot = [sb(f"hot{n}", [P, TILES, EXPERTS]) for n in range(2)]
        weighted = [sb(f"weighted{n}", [P, TILES, EXPERTS]) for n in range(2)]
        gates = sb("gates", [P, TILES, EXPERTS])
        gatesT = sb("gatesT", [EXPERTS, CHUNK])
        gate_rows = [sb(f"gate_rows{n}", [P, EPAIRS, CHUNK]) for n in range(2)]
        silu = [sb(f"silu{n}", [P, CHUNK]) for n in range(SILUS)]
        hid = [sb(f"hid{n}", [P, CHUNK]) for n in range(HIDS)]
        gated = [sb(f"gated{n}", [P, CHUNK]) for n in range(GATED)]
        acc = [sb(f"acc{n}", [P, CHUNK]) for n in range(2)]
        result = [sb(f"result{n}", [P, TILES, E]) for n in range(2)]

        h1_ps = [bank(f"h1_ps{n}") for n in range(2)]
        h2_ps = [bank(f"h2_ps{n}") for n in range(2)]
        y_ps = bank("y_ps")
        tail_ps = bank("tail_ps")
        att_ps = [bank(f"att_ps{n}") for n in range(2)]

        passed = sem("passed")
        small_in = sem("small_in")
        experts_in = sem("experts_in")
        pool_const = sem("pool_const")
        setup_perm = sem("setup_perm")
        setup_turned = sem("setup_turned")
        setup_zero = sem("setup_zero")
        setup_done = sem("setup_done")
        bias_sum = sem("bias_sum")
        split_hi = sem("split_hi")
        experts_ready = sem("experts_ready")
        rows_in = sem("rows_in")
        hx_ps_ready = sem("hx_ps_ready")
        hx_ready = sem("hx_ready")
        sum_done = [sem(f"sum_done{n}") for n in range(2)]
        mean_ready = [sem(f"mean_ready{n}") for n in range(2)]
        centered = [sem(f"centered{n}") for n in range(2)]
        squared = [sem(f"squared{n}") for n in range(2)]
        sq_sum_done = [sem(f"sq_sum_done{n}") for n in range(2)]
        var_ready = [sem(f"var_ready{n}") for n in range(2)]
        rstd_ready = [sem(f"rstd_ready{n}") for n in range(2)]
        normed = [sem(f"normed{n}") for n in range(2)]
        qkv_ps_ready = sem("qkv_ps_ready")
        qkv_copied = sem("qkv_copied")
        qkv_ready = sem("qkv_ready")
        kpart_ready = sem("kpart_ready")
        kpart_turned = sem("kpart_turned")
        kmax_ready = sem("kmax_ready")
        kdiag_ready = sem("kdiag_ready")
        kmax_spread = sem("kmax_spread")
        k_shifted = sem("k_shifted")
        k_exp = sem("k_exp")
        qmax_ready = sem("qmax_ready")
        q_shifted = sem("q_shifted")
        q_exp = sem("q_exp")
        qsum_ready = sem("qsum_ready")
        qinv_ready = sem("qinv_ready")
        q_ready = sem("q_ready")
        ctx_ps_ready = sem("ctx_ps_ready")
        ctx_ready = sem("ctx_ready")
        mix_ps_ready = sem("mix_ps_ready")
        mix_ready = sem("mix_ready")
        q_turned = sem("q_turned")
        qsT_ready = sem("qsT_ready")
        attended = sem("attended")
        h2_ready = sem("h2_ready")
        z_turned = sem("z_turned")
        z_hi = sem("z_hi")
        residual_kept = sem("residual_kept")
        z_split = sem("z_split")
        logits_ps_ready = sem("logits_ps_ready")
        logits_ready = sem("logits_ready")
        top_ready = sem("top_ready")
        top_id_ready = sem("top_id_ready")
        margin_ready = sem("margin_ready")
        tanh_ready = sem("tanh_ready")
        shares_ready = sem("shares_ready")
        hot_ready = sem("hot_ready")
        weighted_ready = sem("weighted_ready")
        gates_ready = sem("gates_ready")
        gates_turned = sem("gates_turned")
        gatesT_ready = sem("gatesT_ready")
        gates_stored = sem("gates_stored")
        gate_rows_in = [sem(f"gate_rows_in{n}") for n in range(2)]
        h1_done = sem("h1_done")
        h2_done = sem("h2_done")
        silu_done = sem("silu_done")
        hid_done = sem("hid_done")
        y_done = sem("y_done")
        gated_done = sem("gated_done")
        acc_done = sem("acc_done")
        folded = sem("folded")
        result_ready = sem("result_ready")
        result_out = [sem(f"result_out{n}") for n in range(2)]

        SMALL_DMAS = 2 + 8 + 2 + 2 + 1 + 6 + 2 + 1
        block = ctx.enter_context(nc.Block())

        def reuse(eng, last_use, count):
            if not isinstance(count, int) or count > 0:
                eng.wait_ge(last_use, count)

        def lone_wait(eng, signal, count):
            eng.wait_ge(signal, count)
            eng.sem_inc(passed, 1)

        def before(m, c):
            return (m, c - 1) if c else (m - 1, CHUNKS - 1)

        def projected(m, k):
            c, e = divmod(k, EXPERTS)
            if e % 2 == 0:
                return None
            if e >= 3:
                return m, c, (e - 3) // 2
            started = c > 0 or not isinstance(m, int) or m > 0
            return (*before(m, c), EPAIRS - 1) if started else None

        def place(c):
            t0 = c % (CHUNKS // 2) * TILES
            return c // (CHUNKS // 2), slice(t0, t0 + TILES)

        def uses(m, c):
            return CHUNKS // 2 * m + c // 2 + 1

        def for_slots(eng, attend, experts):
            for k in range(FIRST, SLOTS):
                attend(0, k)
            for k in range(FIRST):
                experts(0, k)
            for k in range(FIRST, SLOTS):
                experts(0, k)
                attend(1, k)
            for k in range(FIRST):
                experts(1, k)
            with eng.Fori(1, PAIRS - 1) as m:
                for k in range(FIRST, SLOTS):
                    experts(m, k)
                    attend(m + 1, k)
                for k in range(FIRST):
                    experts(m + 1, k)
            for k in range(FIRST, SLOTS):
                experts(PAIRS - 1, k)

        def for_routes(m, k, route):
            for c in range(1, CHUNKS):
                if ROUTE[c] <= k < ROUTE[c] + EXPERTS:
                    route(m, c, k - ROUTE[c])

        @block.sync
        def _(sp):
            def load_rows(m):
                for b in range(2):
                    for i in range(PATCH):
                        row = x[2 * m + b, 0, i, :]
                        src = bass.AP(tensor=row.tensor, offset=row.offset,
                                      ap=[[1, PATCH], [PATCH * FRAMES, MP], [1, SHIFTED]])
                        p0 = b * E + i * PATCH
                        sp.dma_start(rows[p0:p0 + PATCH, :, 0:SHIFTED], src).then_inc(rows_in, 16)

            def spread_gates(m, c):
                n, ring = CHUNKS * m + c, c % 2
                lone_wait(sp, gatesT_ready, n + 1)
                sp.dma_start(gates_dram[ring], gatesT[:, :]).then_inc(gates_stored, 16)
                lone_wait(sp, gates_stored, 16 * (n + 1))
                if not isinstance(n, int) or n > 1:
                    lone_wait(sp, gated_done, EPAIRS * (n - 1))
                for half in range(2):
                    src = gates_dram[ring].rearrange("(q a) t -> a q t", a=2)[half]
                    sp.dma_start(gate_rows[ring][half * E:(half + 1) * E, :, :],
                                 src.partition_broadcast(E)).then_inc(gate_rows_in[ring], 16)

            def store(m, c):
                b, blocks = place(c)
                lone_wait(sp, result_ready, CHUNKS * m + c + 1)
                dst = out[2 * m + b, blocks.start * P:blocks.stop * P, :].rearrange("(t s) e -> s t e", s=P)
                sp.dma_start(dst, result[c % 2][:, :, :]).then_inc(result_out[c % 2], 16)

            def pair(m, more_rows, more_gates):
                spread_gates(m, 1)
                store(m, 0)
                spread_gates(m, 2)
                store(m, 1)
                spread_gates(m, 3)
                if more_rows:
                    lone_wait(sp, attended, 2 * m + 4)
                    load_rows(m + 2)
                if more_gates:
                    spread_gates(m + 1, 0)
                store(m, 2)
                store(m, 3)

            def small(dst, src):
                sp.dma_start(dst, src).then_inc(small_in, 16)

            for d in range(2):
                small(tok_w_in[:, d, :], tok_w)
            load_rows(0)
            for n, w in enumerate((wq, wk, wv, wr)):
                for d in range(2):
                    small(proj_in[:, n, d, :], w)
            small(emb_bias[:, :], tok_b.partition_broadcast(P))
            small(out_bias[:, :], br.partition_broadcast(P))
            for d in range(2):
                small(pos_chan[d * E:(d + 1) * E, :, :], pos[0].rearrange("(c r) e -> c r e", r=ROWS))
            small(pos_tok[:, :, :], pos[0].rearrange("(t s) e -> s t e", s=P))
            for n, bias in enumerate((bq, bk, bv)):
                for d in range(2):
                    small(qkv_bias[:, n, d, :], bias.partition_broadcast(P))
            for d in range(2):
                small(gate_in[d * E:(d + 1) * E, :], gate_w)
            small(gate_bias[:, :], gate_b.partition_broadcast(P))
            for ring, w in enumerate((w1, w2)):
                for d in range(2):
                    raw = gate_rows[ring][d * E:(d + 1) * E, 0:4, :].rearrange("p a (b h) -> p (a b) h", h=HIDDEN)
                    sp.dma_start(raw, w.rearrange("e d h -> d e h")).then_inc(experts_in, 16)
            sp.dma_start(w3_sb[:, :, :], w3.rearrange("e h d -> h e d")).then_inc(experts_in, 16)

            sp.wait_ge(attended, 2)
            load_rows(1)
            sp.wait_ge(experts_ready, 2)
            spread_gates(0, 0)
            pair(0, True, True)
            with sp.Fori(1, PAIRS - 2) as m:
                pair(m, True, True)
            pair(PAIRS - 2, False, True)
            pair(PAIRS - 1, False, False)
            for n in range(2):
                sp.wait_ge(result_out[n], 16 * PAIRS * CHUNKS // 2)

        @block.gpsimd
        def _(pool):
            gp = nc.gpsimd
            gp.memset(ident[:, :], 0.0).then_inc(pool_const, 1)
            gp.memset(fold[:, :], 0.0).then_inc(pool_const, 1)
            gp.memset(head_mask[:, :], 1.0).then_inc(pool_const, 1)
            gp.memset(ones[:, :], 1.0).then_inc(pool_const, 1)
            gp.memset(minus_half[:, :], -0.5).then_inc(pool_const, 1)
            gp.iota(expert_id[:, :], [[1, EXPERTS]], base=0, channel_multiplier=0,
                    allow_small_or_imprecise_dtypes=True).then_inc(pool_const, 1)
            pool.wait_ge(pool_const, 6)
            gp.affine_select(out=ident[:, :], in_=ident[:, :], compare_op=ALU.not_equal, fill=1.0,
                             base=0, pattern=[[-1, P]], channel_multiplier=1).then_inc(pool_const, 1)
            gp.affine_select(out=fold[:, :], in_=fold[:, :], compare_op=ALU.not_equal, fill=1.0,
                             base=0, pattern=[[-1, E]], channel_multiplier=1).then_inc(pool_const, 1)
            hm = head_mask[:, :].rearrange("p (g j) -> p g j", j=HEAD)
            gp.affine_select(out=hm, in_=hm, compare_op=ALU.is_ge, fill=0.0,
                             base=0, pattern=[[-HEAD, P // HEAD], [0, HEAD]], channel_multiplier=1).then_inc(pool_const, 1)
            pool.wait_ge(pool_const, 9)
            gp.affine_select(out=fold[:, :], in_=fold[:, :], compare_op=ALU.not_equal, fill=1.0,
                             base=-E, pattern=[[-1, E]], channel_multiplier=1).then_inc(pool_const, 1)
            gp.affine_select(out=hm, in_=hm, compare_op=ALU.is_ge, fill=0.0,
                             base=HEAD - 1, pattern=[[HEAD, P // HEAD], [0, HEAD]], channel_multiplier=-1).then_inc(pool_const, 1)
            pool.wait_ge(small_in, 16 * SMALL_DMAS)

            hx_groups = hx[:, :].rearrange("p (g e) -> p g e", e=E)
            h2_groups = h2[:, :, :, :].rearrange("p t b e -> p (t b) e")
            z_groups = z[:, :, :, :].rearrange("p t b e -> p (t b) e")
            q_heads = qkv[:, :, 0:P].rearrange("p t (g j) -> p t g j", j=HEAD)

            def norm_center(ln, m, dst, src):
                pool.wait_ge(mean_ready[ln], m + 1)
                mean = stats[ln][1][:, :].unsqueeze(2).broadcast_to([P, 2 * BLOCKS, E])
                gp.tensor_tensor(dst, src, mean, ALU.subtract).then_inc(centered[ln], 1)

            def norm_scale(ln, m, data):
                pool.wait_ge(var_ready[ln], m + 1)
                gp.tensor_tensor(stats[ln][4][:, :], stats[ln][3][:, :], minus_half[:, :],
                                 ALU.pow).then_inc(rstd_ready[ln], 1)
                pool.wait_ge(rstd_ready[ln], m + 1)
                rstd = stats[ln][4][:, :].unsqueeze(2).broadcast_to([P, 2 * BLOCKS, E])
                gp.tensor_tensor(data, data, rstd, ALU.mult).then_inc(normed[ln], 1)

            def attend(m, k):
                if k == CENTER1:
                    norm_center(0, m, hx_groups, hx_groups)
                if k == SCALE1:
                    norm_scale(0, m, hx_groups)
                if QKV + 1 <= k < QKV + 1 + BLOCKS:
                    t = k - QKV - 1
                    pool.wait_ge(qkv_copied, BLOCKS * m + t + 1)
                    gp.tensor_tensor(qkv[:, t, :], qkv[:, t, :], qkv_bias[:, :, :, :].rearrange("p n d e -> p (n d e)"),
                                     ALU.add).then_inc(qkv_ready, 1)
                if k == QCENTER:
                    pool.wait_ge(qmax_ready, m + 1)
                    gp.tensor_tensor(q_heads, q_heads, qmax[:, :, :].unsqueeze(3).broadcast_to([P, BLOCKS, P // HEAD, HEAD]),
                                     ALU.subtract).then_inc(q_shifted, 1)
                if k == QSCALE:
                    pool.wait_ge(qinv_ready, m + 1)
                    gp.tensor_tensor(q_heads, q_heads, qinv[:, :, :].unsqueeze(3).broadcast_to([P, BLOCKS, P // HEAD, HEAD]),
                                     ALU.mult).then_inc(q_ready, 1)
                if k == CENTER2:
                    reuse(pool, z_turned, CHUNKS * m)
                    norm_center(1, m, z_groups, h2_groups)
                if k == SCALE2:
                    norm_scale(1, m, z_groups)

            def accumulate(m, c, q):
                n = CHUNKS * m + c
                pool.wait_ge(gated_done, EPAIRS * n + q + 1)
                if q > 1:
                    pool.wait_ge(acc_done, (EPAIRS - 1) * n + q - 1)
                gp.tensor_tensor(acc[c % 2][:, :], acc[c % 2][:, :], gated[q % GATED][:, :],
                                 ALU.add).then_inc(acc_done, 1)

            def experts(m, k):
                at = projected(m, k)
                if at and at[2] > 0:
                    accumulate(*at)

            for_slots(pool, attend, experts)
            accumulate(PAIRS - 1, CHUNKS - 1, EPAIRS - 1)

        @block.scalar
        def _(act):
            sc = nc.scalar

            def route(m, c, step):
                n = CHUNKS * m + c
                b, blocks = place(c)
                if step == 0:
                    act.wait_ge(z_turned, n + 1)
                    reuse(act, h2_done, EXPERTS * (n - 1))
                    sc.activation(zs[c % 2][0:E, :], tail_ps[0:E, :], ACT.Copy).then_inc(z_hi, 1)
                    reuse(act, result_ready, n - CHUNKS + 1)
                    sc.activation(residual[c][:, :, :], h2[:, blocks, b, :], ACT.Copy).then_inc(residual_kept, 1)
                if step == 4:
                    act.wait_ge(margin_ready, n + 1)
                    reuse(act, shares_ready, 2 * n)
                    sc.activation(half_tanh[:, :], margin[:, :], ACT.Tanh, scale=0.5).then_inc(tanh_ready, 1)
                if step == 7:
                    act.wait_ge(gates_turned, n + 1)
                    reuse(act, gates_stored, 16 * n)
                    sc.activation(gatesT[:, :], tail_ps[0:EXPERTS, :], ACT.Copy).then_inc(gatesT_ready, 1)

            def attend(m, k):
                if k == SQUARE1:
                    act.wait_ge(centered[0], m + 1)
                    reuse(act, sq_sum_done[1], m)
                    sc.activation(squares[:, :], hx[:, :], ACT.Square).then_inc(squared[0], 1)
                if QKV <= k < QKV + BLOCKS:
                    t = k - QKV
                    act.wait_ge(qkv_ps_ready, BLOCKS * m + t + 1)
                    reuse(act, q_turned, 2 * m)
                    sc.activation(qkv[:, t, :], att_ps[t % 2][:, 0:3 * P], ACT.Copy).then_inc(qkv_copied, 1)
                if k == EXPS:
                    act.wait_ge(k_shifted, m + 1)
                    sc.activation(qkv[:, :, P:2 * P], qkv[:, :, P:2 * P], ACT.Exp).then_inc(k_exp, 1)
                    act.wait_ge(q_shifted, m + 1)
                    sc.activation(qkv[:, :, 0:P], qkv[:, :, 0:P], ACT.Exp).then_inc(q_exp, 1)
                if k in (QTURN, QTURN + 1):
                    u = k - QTURN
                    act.wait_ge(q_turned, 2 * m + u + 1)
                    reuse(act, attended, 2 * m)
                    sc.activation(qsT[:, u * CHUNK:(u + 1) * CHUNK], att_ps[u][:, :], ACT.Copy).then_inc(qsT_ready, 1)
                if k == SQUARE2:
                    act.wait_ge(centered[1], m + 1)
                    sc.activation(squares[:, :], z[:, :, :, :].rearrange("p t b e -> p (t b e)"),
                                  ACT.Square).then_inc(squared[1], 1)
                if k >= ROUTE[0]:
                    route(m, 0, k - ROUTE[0])

            def experts(m, k):
                g = SLOTS * m + k
                act.wait_ge(h1_done, g + 1)
                reuse(act, hid_done, g - SILUS + 1)
                sc.activation(silu[k % SILUS][:, :], h1_ps[k % 2][:, :], ACT.Silu).then_inc(silu_done, 1)
                for_routes(m, k, route)

            for_slots(act, attend, experts)

        @block.vector
        def _(dve):
            ve = nc.vector
            hx_groups = hx[:, :].rearrange("p (g e) -> p g e", e=E)
            h2_groups = h2[:, :, :, :].rearrange("p t b e -> p (t b) e")
            q_heads = qkv[:, :, 0:P].rearrange("p t (g j) -> p t g j", j=HEAD)
            keys = qkv[:, :, P:2 * P]

            ve.memset(proj[:, :, :], 0.0).then_inc(setup_zero, 1)
            ve.memset(tok_w_both[:, :], 0.0).then_inc(setup_zero, 1)
            dve.wait_ge(small_in, 16 * SMALL_DMAS)
            ve.tensor_copy(tok_w_perm[:, :], tok_w_in[:, :, :].rearrange("e d k -> e (d k)")).then_inc(setup_perm, 1)
            ve.tensor_tensor(pos_chan[:, :, :], pos_chan[:, :, :],
                             emb_bias[:, :].unsqueeze(1).broadcast_to([P, ROWS, E]), ALU.add).then_inc(setup_done, 1)
            ve.tensor_tensor(out_bias[:, :], out_bias[:, :], emb_bias[:, :], ALU.add).then_inc(bias_sum, 1)
            ve.tensor_copy(gate_hi[:, :], gate_in[:, :]).then_inc(split_hi, 1)
            dve.wait_ge(bias_sum, 1)
            ve.tensor_tensor(pos_tok[:, :, :], pos_tok[:, :, :],
                             out_bias[:, :].unsqueeze(1).broadcast_to([P, BLOCKS, E]), ALU.add).then_inc(setup_done, 1)
            dve.wait_ge(split_hi, 1)
            ve.tensor_tensor(gate_lo[:, :], gate_in[:, :], gate_hi[:, :].bitcast(F32), ALU.subtract).then_inc(setup_done, 1)
            dve.wait_ge(setup_turned, 2)
            dve.wait_ge(setup_zero, 2)
            ve.tensor_copy(tok_wT[:, :], att_ps[0][:, 0:E]).then_inc(setup_done, 1)
            turned = att_ps[1][:, 0:4 * E].rearrange("p (n e) -> p n e", n=4)
            for d in range(2):
                ve.tensor_copy(proj[d * E:(d + 1) * E, :, d * E:(d + 1) * E],
                               turned[d * E:(d + 1) * E]).then_inc(setup_done, 1)
                ve.tensor_copy(tok_w_both[d * E:(d + 1) * E, d * E:(d + 1) * E],
                               att_ps[0][d * E:(d + 1) * E, 0:E]).then_inc(setup_done, 1)

            def split_experts():
                dve.wait_ge(experts_in, 16 * 5)
                raws = [r[:, 0:4, :].rearrange("p a (b h) -> p (a b) h", h=HIDDEN) for r in gate_rows]
                for raw, hi in zip(raws, (w1_hi, w2_hi)):
                    ve.tensor_copy(hi[:, :, :], raw).then_inc(split_hi, 1)
                dve.wait_ge(split_hi, 3)
                for raw, hi, lo in zip(raws, (w1_hi, w2_hi), (w1_lo, w2_lo)):
                    ve.tensor_tensor(lo[:, :, :], raw, hi[:, :, :].bitcast(F32), ALU.subtract).then_inc(experts_ready, 1)

            def norm_sum(ln, m, data):
                ve.tensor_reduce(stats[ln][0][:, :], data, AX_X, ALU.add).then_inc(sum_done[ln], 1)
                dve.wait_ge(sum_done[ln], m + 1)
                ve.tensor_scalar(stats[ln][1][:, :], stats[ln][0][:, :], 1.0 / E, None, ALU.mult).then_inc(mean_ready[ln], 1)

            def norm_var(ln, m):
                dve.wait_ge(squared[ln], m + 1)
                ve.tensor_reduce(stats[ln][2][:, :], squares[:, :].rearrange("p (g e) -> p g e", e=E),
                                 AX_X, ALU.add).then_inc(sq_sum_done[ln], 1)
                dve.wait_ge(sq_sum_done[ln], m + 1)
                ve.tensor_scalar(stats[ln][3][:, :], stats[ln][2][:, :], 1.0 / E, EPS,
                                 ALU.mult, ALU.add).then_inc(var_ready[ln], 1)

            def attend(m, k):
                if k in (PATCHES, PATCHES + 1):
                    u = k - PATCHES
                    dve.wait_ge(hx_ps_ready, 2 * m + u + 1)
                    reuse(dve, attended, 2 * m)
                    half = slice(u * ROWS // 2, (u + 1) * ROWS // 2)
                    ve.tensor_tensor(hx[:, u * CHUNK:(u + 1) * CHUNK], att_ps[u][:, :],
                                     pos_chan[:, half, :].rearrange("p r e -> p (r e)"), ALU.add).then_inc(hx_ready, 1)
                if k == MEAN1:
                    dve.wait_ge(hx_ready, 2 * m + 2)
                    norm_sum(0, m, hx_groups)
                if k == VAR1:
                    norm_var(0, m)
                if k == MAXIMA:
                    dve.wait_ge(qkv_ready, BLOCKS * (m + 1))
                    ve.tensor_reduce(kpart[:, :], keys.rearrange("p t c -> p c t"), AX_X, ALU.max).then_inc(kpart_ready, 1)
                    ve.tensor_reduce(qmax[:, :, :], q_heads, AX_X, ALU.max).then_inc(qmax_ready, 1)
                if k == KMAX:
                    dve.wait_ge(kpart_turned, m + 1)
                    ve.tensor_reduce(kmax[:, :], att_ps[0][:, 0:P], AX_X, ALU.max).then_inc(kmax_ready, 1)
                    dve.wait_ge(kmax_ready, m + 1)
                    ve.tensor_scalar(kdiag[:, :], ident[:, :], kmax[:, 0:1], None, ALU.mult).then_inc(kdiag_ready, 1)
                if k == KSUB:
                    dve.wait_ge(kmax_spread, m + 1)
                    ve.tensor_tensor(keys, keys, att_ps[1][:, 0:P].unsqueeze(1).broadcast_to([P, BLOCKS, P]),
                                     ALU.subtract).then_inc(k_shifted, 1)
                if k == QSUM:
                    dve.wait_ge(q_exp, m + 1)
                    ve.tensor_reduce(qsum[:, :, :], q_heads, AX_X, ALU.add).then_inc(qsum_ready, 1)
                    dve.wait_ge(qsum_ready, m + 1)
                    ve.reciprocal(qinv[:, :, :], qsum[:, :, :]).then_inc(qinv_ready, 1)
                if k == CMASK:
                    dve.wait_ge(ctx_ps_ready, m + 1)
                    ve.tensor_tensor(ctxT[:, :], att_ps[0][:, 0:P], head_mask[:, :], ALU.mult).then_inc(ctx_ready, 1)
                    ve.reciprocal(kinv[:, :], att_ps[0][:, P:P + 1]).then_inc(ctx_ready, 1)
                if k == MSCALE:
                    dve.wait_ge(mix_ps_ready, m + 1)
                    dve.wait_ge(ctx_ready, 2 * m + 2)
                    ve.tensor_scalar(mix[:, :], att_ps[1][:, 0:P], kinv[:, 0:1], None, ALU.mult).then_inc(mix_ready, 1)
                if k in (ATTENDED, ATTENDED + 1):
                    u = k - ATTENDED
                    dve.wait_ge(attended, 2 * m + u + 1)
                    reuse(dve, residual_kept, CHUNKS * m)
                    half = slice(u * TILES, (u + 1) * TILES)
                    for b in range(2):
                        ve.tensor_tensor(h2[:, half, b, :],
                                         att_ps[u][:, :].rearrange("p (t b e) -> p t b e", t=TILES, b=2)[:, :, b, :],
                                         pos_tok[:, half, :], ALU.add).then_inc(h2_ready, 1)
                if k == MEAN2:
                    dve.wait_ge(h2_ready, 4 * m + 4)
                    norm_sum(1, m, h2_groups)
                if k == VAR2:
                    norm_var(1, m)
                if k >= ROUTE[0]:
                    route(m, 0, k - ROUTE[0])

            def route(m, c, step):
                n = CHUNKS * m + c
                if step == 1:
                    dve.wait_ge(z_hi, n + 1)
                    ve.tensor_tensor(zs[c % 2][E:P, :], tail_ps[0:E, :], zs[c % 2][0:E, :].bitcast(F32),
                                     ALU.subtract).then_inc(z_split, 1)
                if step == 2:
                    dve.wait_ge(logits_ps_ready, n + 1)
                    ve.tensor_tensor(logits[:, :, :], tail_ps[:, 0:TILES * EXPERTS].rearrange("p (t e) -> p t e", e=EXPERTS),
                                     gate_bias[:, :].unsqueeze(1).broadcast_to([P, TILES, EXPERTS]),
                                     ALU.add).then_inc(logits_ready, 1)
                if step == 3:
                    lone_wait(dve, logits_ready, n + 1)
                    for j in range(TILES):
                        ve.max(top[:, j, :], logits[:, j, :]).then_inc(top_ready, 1)
                    dve.wait_ge(top_ready, TILES * (n + 1))
                    reuse(dve, tanh_ready, n)
                    ve.tensor_tensor(margin[:, :], top[:, :, 0], top[:, :, 1], ALU.subtract).then_inc(margin_ready, 1)
                    for j in range(TILES):
                        ve.max_index(top_id[:, j, :], top[:, j, :], logits[:, j, :]).then_inc(top_id_ready, 1)
                if step == 4:
                    dve.wait_ge(top_id_ready, TILES * (n + 1))
                    for r in range(2):
                        ve.tensor_tensor(hot[r][:, :, :], expert_id[:, :].unsqueeze(1).broadcast_to([P, TILES, EXPERTS]),
                                         top_id[:, :, r].unsqueeze(2).broadcast_to([P, TILES, EXPERTS]),
                                         ALU.is_equal).then_inc(hot_ready, 1)
                    dve.wait_ge(tanh_ready, n + 1)
                    for r in range(2):
                        ve.tensor_scalar(share[r][:, :], half_tanh[:, :], 0.5 - r, 0.5, ALU.mult, ALU.add).then_inc(shares_ready, 1)
                if step == 5:
                    dve.wait_ge(hot_ready, 2 * (n + 1))
                    dve.wait_ge(shares_ready, 2 * (n + 1))
                    for r in range(2):
                        ve.tensor_tensor(weighted[r][:, :, :], hot[r][:, :, :],
                                         share[r][:, :].unsqueeze(2).broadcast_to([P, TILES, EXPERTS]),
                                         ALU.mult).then_inc(weighted_ready, 1)
                    dve.wait_ge(weighted_ready, 2 * (n + 1))
                    reuse(dve, gates_turned, n)
                    ve.tensor_tensor(gates[:, :, :], weighted[0][:, :, :], weighted[1][:, :, :],
                                     ALU.add).then_inc(gates_ready, 1)

            def weigh(m, c, q):
                n = CHUNKS * m + c
                others = EPAIRS - 1
                dve.wait_ge(y_done, EPAIRS * n + q + 1)
                if q == 0:
                    dve.wait_ge(gate_rows_in[c % 2], 32 * uses(m, c))
                    reuse(dve, folded, n - 1)
                    dst = acc[c % 2]
                else:
                    reuse(dve, acc_done, others * n + q - GATED if q > GATED else others * (n - 1) + min(q + GATED, q % GATED + 4))
                    dst = gated[q % GATED]
                ve.tensor_tensor(dst[:, :], y_ps[:, :], gate_rows[c % 2][:, q, :], ALU.mult).then_inc(gated_done, 1)

            def finish(m, c):
                dve.wait_ge(folded, CHUNKS * m + c + 1)
                reuse(dve, result_out[c % 2], 16 * (uses(m, c) - 1))
                ve.tensor_tensor(result[c % 2][:, :, :], tail_ps[:, 0:TILES * E].rearrange("p (t e) -> p t e", e=E),
                                 residual[c][:, :, :], ALU.add).then_inc(result_ready, 1)

            def experts(m, k):
                c, e = divmod(k, EXPERTS)
                g = SLOTS * m + k
                started = c > 0 or not isinstance(m, int) or m > 0
                dve.wait_ge(silu_done, g + 1)
                dve.wait_ge(h2_done, g + 1)
                reuse(dve, y_done, SLOTS // 2 * m + (k - HIDS) // 2 + 1)
                ve.tensor_tensor(hid[k % HIDS][:, :], silu[k % SILUS][:, :], h2_ps[k % 2][:, :], ALU.mult).then_inc(hid_done, 1)
                if at := projected(m, k):
                    weigh(*at)
                if e == FOLD[c] and started:
                    finish(*before(m, c))
                for_routes(m, k, route)

            def attend_first(m, k):
                attend(m, k)
                if isinstance(m, int) and m == 0 and k == QKV:
                    split_experts()

            for_slots(dve, attend_first, experts)
            weigh(PAIRS - 1, CHUNKS - 1, EPAIRS - 1)
            finish(PAIRS - 1, CHUNKS - 1)

        @block.tensor
        def _(pe):
            te = nc.tensor
            samples = rows[:, :, :].rearrange("p m f -> p (m f)")
            pe.wait_ge(pool_const, 11)
            pe.wait_ge(setup_perm, 1)
            te.transpose(att_ps[0][:, 0:E], tok_w_perm[:, :], ident[0:E, 0:E]).then_inc(setup_turned, 1)
            for n in range(4):
                mm = te.transpose(att_ps[1][:, n * E:(n + 1) * E], proj_in[:, n, :, :].rearrange("o d c -> o (d c)"),
                                  ident[0:E, 0:E])
            mm.then_inc(setup_turned, 1)
            pe.wait_ge(setup_done, 8)

            def attend(m, k):
                if k in (PATCHES, PATCHES + 1):
                    u = k - PATCHES
                    reuse(pe, h2_ready, 4 * m - 2 + 2 * u)
                    lone_wait(pe, rows_in, 16 * 2 * PATCH * (m + 1))
                    for r in range(ROWS // 2):
                        for b in range(2):
                            img = slice(b * E, (b + 1) * E)
                            at = PATCH * (u * ROWS // 2 + r)
                            cols = samples[img, at:at + PATCH * ROWS * (E - 1) + 1:PATCH * ROWS]
                            mm = te.matmul(att_ps[u][img, r * E:(r + 1) * E], cols, tok_wT[img, :], start=True, stop=True)
                    mm.then_inc(hx_ps_ready, 1)
                if QKV <= k < QKV + BLOCKS:
                    t = k - QKV
                    pe.wait_ge(normed[0], m + 1)
                    if t >= 2:
                        pe.wait_ge(qkv_copied, BLOCKS * m + t - 1)
                    te.matmul(att_ps[t % 2][:, 0:3 * P], hx[:, t * P:(t + 1) * P],
                              proj[:, 0:3, :].rearrange("p n o -> p (n o)"), start=True, stop=True).then_inc(qkv_ps_ready, 1)
                if k == KTURN:
                    pe.wait_ge(kpart_ready, m + 1)
                    te.transpose(att_ps[0][:, 0:P], kpart[:, :], ident[:, :]).then_inc(kpart_turned, 1)
                if k == KSPREAD:
                    pe.wait_ge(kdiag_ready, m + 1)
                    te.matmul(att_ps[1][:, 0:P], ones[:, :], kdiag[:, :], start=True, stop=True).then_inc(kmax_spread, 1)
                if k == CONTEXT:
                    pe.wait_ge(k_exp, m + 1)
                    for t in range(BLOCKS):
                        te.matmul(att_ps[0][:, 0:P], qkv[:, t, 2 * P:3 * P], qkv[:, t, P:2 * P],
                                  start=(t == 0), stop=(t == BLOCKS - 1))
                    for t in range(BLOCKS):
                        mm = te.matmul(att_ps[0][:, P:P + 1], qkv[:, t, P:2 * P], ones[:, 0:1],
                                       start=(t == 0), stop=(t == BLOCKS - 1))
                    mm.then_inc(ctx_ps_ready, 1)
                if k == MIX:
                    pe.wait_ge(ctx_ready, 2 * m + 2)
                    te.matmul(att_ps[1][:, 0:P], ctxT[:, :], proj[:, 3, :], start=True, stop=True).then_inc(mix_ps_ready, 1)
                if k in (QTURN, QTURN + 1):
                    u = k - QTURN
                    pe.wait_ge(q_ready, m + 1)
                    pe.wait_ge(mix_ready, m + 1)
                    for j in range(TILES):
                        mm = te.transpose(att_ps[u][:, j * P:(j + 1) * P], qkv[:, u * TILES + j, 0:P], ident[:, :])
                    mm.then_inc(q_turned, 1)
                if k in (ATTENDED, ATTENDED + 1):
                    u = k - ATTENDED
                    pe.wait_ge(qsT_ready, 2 * m + 2)
                    for j in range(TILES):
                        t = u * TILES + j
                        o = att_ps[u][:, j * P:(j + 1) * P]
                        te.matmul(o, qsT[:, t * P:(t + 1) * P], mix[:, :], start=True, stop=False)
                        te.matmul(o, hx[:, t * P:(t + 1) * P], ident[:, :], start=False, stop=False)
                        cols = samples[:, PATCH * P * t:PATCH * (P * (t + 1) - 1) + 1:PATCH]
                        mm = te.matmul(o, cols, tok_w_both[:, :], start=False, stop=True)
                    mm.then_inc(attended, 1)
                if k >= ROUTE[0]:
                    route(m, 0, k - ROUTE[0])

            def route(m, c, step):
                n = CHUNKS * m + c
                b, blocks = place(c)
                if step == 0:
                    if not isinstance(n, int) or n > 0:
                        pe.wait_ge(gatesT_ready, n)
                    if c == 1:
                        reuse(pe, result_ready, n - 2)
                    lone_wait(pe, normed[1], m + 1)
                    for j in range(TILES):
                        mm = te.transpose(tail_ps[0:E, j * P:(j + 1) * P], z[:, blocks.start + j, b, :], ident[:, :])
                    mm.then_inc(z_turned, 1)
                if step == 2:
                    pe.wait_ge(z_split, n + 1)
                    for j in range(TILES):
                        o = tail_ps[:, j * EXPERTS:(j + 1) * EXPERTS]
                        te.matmul(o, zs[c % 2][:, j * P:(j + 1) * P], gate_hi[:, :], start=True, stop=False)
                        mm = te.matmul(o, zs[c % 2][:, j * P:(j + 1) * P], gate_lo[:, :], start=False, stop=True)
                    mm.then_inc(logits_ps_ready, 1)
                if step == 6:
                    pe.wait_ge(gates_ready, n + 1)
                    if c > 0:
                        reuse(pe, result_ready, n - 1)
                    for j in range(TILES):
                        mm = te.transpose(tail_ps[0:EXPERTS, j * P:(j + 1) * P], gates[:, j, :], ident[:, :])
                    mm.then_inc(gates_turned, 1)

            def project(m, c, q):
                n = CHUNKS * m + c
                pe.wait_ge(hid_done, EXPERTS * n + 2 * q + 2)
                reuse(pe, gated_done, EPAIRS * n + q)
                for a in range(2):
                    e = 2 * q + a
                    mm = te.matmul(y_ps[a * E:(a + 1) * E, :], w3_sb[:, e, :], hid[e % HIDS][:, :], start=True, stop=True)
                mm.then_inc(y_done, 1)

            def fold_sum(m, c, reader, count):
                pe.wait_ge(acc_done, (EPAIRS - 1) * (CHUNKS * m + c + 1))
                pe.wait_ge(reader, count)
                for j in range(TILES):
                    mm = te.matmul(tail_ps[:, j * E:(j + 1) * E], acc[c % 2][:, j * P:(j + 1) * P], fold[:, :],
                                   start=True, stop=True)
                mm.then_inc(folded, 1)

            def experts(m, k):
                c, e = divmod(k, EXPERTS)
                n, g = CHUNKS * m + c, SLOTS * m + k
                started = c > 0 or not isinstance(m, int) or m > 0
                if e == 0:
                    pe.wait_ge(z_split, n + 1)
                    if isinstance(m, int) and m == 0 and c == 0:
                        pe.wait_ge(experts_ready, 2)
                        pe.wait_ge(experts_in, 16 * 5)
                for hi, lo, banks, reader, done in ((w1_hi, w1_lo, h1_ps, silu_done, h1_done),
                                                    (w2_hi, w2_lo, h2_ps, hid_done, h2_done)):
                    reuse(pe, reader, g - 1)
                    te.matmul(banks[k % 2][:, :], hi[:, e, :], zs[c % 2][:, :], start=True, stop=False)
                    te.matmul(banks[k % 2][:, :], lo[:, e, :], zs[c % 2][:, :], start=False, stop=True).then_inc(done, 1)
                if at := projected(m, k):
                    project(*at)
                if e == FOLD[c] and started:
                    if c < CHUNKS - 1:
                        fold_sum(*before(m, c), logits_ready, n + 2)
                    else:
                        fold_sum(*before(m, c), gatesT_ready, n + 1 if isinstance(m, int) and m == PAIRS - 1 else n + 2)
                for_routes(m, k, route)

            for_slots(pe, attend, experts)
            project(PAIRS - 1, CHUNKS - 1, EPAIRS - 1)
            fold_sum(PAIRS - 1, CHUNKS - 1, result_ready, CHUNKS * PAIRS - 1)


_INS = ["x", "L0_tok_W", "L0_tok_b", "L0_tok_pos_embed", "L0_attn_Wk", "L0_attn_bk", "L0_attn_Wq", "L0_attn_bq",
        "L0_attn_Wv", "L0_attn_bv", "L0_attn_Wr", "L0_attn_br", "L0_ffn_gate_w", "L0_ffn_gate_b",
        "L0_ffn_w1", "L0_ffn_w2", "L0_ffn_w3"]


def kernel(**inputs):
    import numpy as np
    import concourse.bacc as bacc
    from concourse.bass_utils import run_bass_kernel_spmd

    nc = bacc.Bacc("TRN2", target_bir_lowering=False, num_devices=1)
    arrays, args = {}, []
    for name in _INS:
        a = np.ascontiguousarray(inputs[name])
        arrays[f"in_{name}"] = a
        args.append(nc.dram_tensor(f"in_{name}", a.shape, mybir.dt.from_np(a.dtype), kind="ExternalInput").ap())
    out = nc.dram_tensor("out_0", (IMAGES, TOKENS, E), F32, kind="ExternalOutput").ap()
    vit_kernel(nc, *args, out)
    r = run_bass_kernel_spmd(nc, [arrays], core_ids=[0])
    return r.results[0]["out_0"]
```

```python
from contextlib import ExitStack

import concourse.bass as bass
from concourse import mybir

F32 = mybir.dt.float32
F32R = mybir.dt.float32r
U32 = mybir.dt.uint32
ACT = mybir.ActivationFunctionType
ALU = mybir.AluOpType
AX_X = mybir.AxisListType.X

P = 128
IMAGES, MELS, FRAMES = 16, 128, 512
PATCH = 8
E = 64
MP, FP = MELS // PATCH, FRAMES // PATCH
TOKENS = MP * FP
ROWS = TOKENS // E
HEAD = 8
EXPERTS, HIDDEN = 16, 128
EPS = 1e-5
PAIRS = IMAGES // 2
BLOCKS = TOKENS // P
CHUNK = 512
TILES = CHUNK // P
CHUNKS = 2 * TOKENS // CHUNK
SLOTS = CHUNKS * EXPERTS
EPAIRS = EXPERTS // 2
SHIFTED = FRAMES - PATCH + 1
SILUS, HIDS, GATED = 4, 4, 4
EARLY = 2

EMBED, ADD1, ADD_BIAS = 0, (0, 1), (26, 27)
MEAN1, CENTER1, SQUARE1, VAR1, SCALE1 = (7, 9), (8, 9), (9, 11), (10, 12), (10, 11)
QKV = tuple(range(14, 22))
QKV_OUT = QKV
KPART, KTURN, KMAX, KSPREAD, KSUB = (19, 23), 26, 25, 27, (28, 29)
QMAX, QCENTER = (20, 25), (23, 24)
EXPS, KSUM, CONTEXT, CMASK, MIX, MSCALE = 31, 32, 33, 33, 35, 36
QSUM, QSCALE, QTURN = (33, 34), (33, 35), (38, 39)
ATTENDED, ADD2 = (40, 42), (40, 42)
MEAN2, CENTER2, SQUARE2, VAR2, SCALE2 = (41, 42), (41, 44), (42, 47), (45, 47), (46, 49)
ROUTE = {1: 0, 2: 16, 3: 33, 0: 51}
Z_TURN, Z_HI, Z_LO, LOGITS, LOGITS_OUT = 0, 0, 0, 3, 3
TOP, SHARES, GATES, GATES_TURN, GATES_OUT = 4, 5, 6, 8, 8
FOLD = {0: 5, 1: 5, 2: 7, 3: 12}
FINISH = {0: 5, 1: 5, 2: 7, 3: 11}


def vit_kernel(nc, x, tok_w, tok_b, pos, wk, bk, wq, bq, wv, bv, wr, br, gate_w, gate_b, w1, w2, w3, out):
    embed_dram = nc.dram_tensor("embed_scratch", (2, TOKENS, E), F32, kind="Internal").ap()
    gates_dram = nc.dram_tensor("gates_scratch", (2, EXPERTS, CHUNK), F32, kind="Internal").ap()
    with ExitStack() as ctx:
        def sb(name, shape, dt=F32):
            return ctx.enter_context(nc.sbuf_tensor(name, shape, dt))

        def bank(name):
            return ctx.enter_context(nc.psum_tensor(name, [P, 512], F32))

        def sem(name):
            return ctx.enter_context(nc.semaphore(name))

        ident = sb("ident", [P, P])
        fold = sb("fold", [P, E])
        ones = sb("ones", [P, P])
        head_mask = sb("head_mask", [P, P])
        tok_w_in = sb("tok_w_in", [E, 2, E])
        tok_w_perm = sb("tok_w_perm", [E, 2 * E])
        tok_w_both = sb("tok_w_both", [P, P])
        proj_in = sb("proj_in", [E, 4, 2, E])
        proj = sb("proj", [P, 4, P])
        qkv_bias = sb("qkv_bias", [P, 3, 2, E])
        emb_bias = sb("emb_bias", [P, E])
        out_bias = sb("out_bias", [P, E])
        pos_tok = sb("pos_tok", [P, BLOCKS, E])
        gate_in = sb("gate_in", [P, EXPERTS])
        gate_split = sb("gate_split", [P, 2, EXPERTS], F32R)
        gate_bias = sb("gate_bias", [P, EXPERTS])
        expert_id = sb("expert_id", [P, EXPERTS])
        minus_half = sb("minus_half", [P, BLOCKS])
        w1_hi = sb("w1_hi", [P, EXPERTS, HIDDEN], F32R)
        w1_lo = sb("w1_lo", [P, EXPERTS, HIDDEN], F32R)
        w2_hi = sb("w2_hi", [P, EXPERTS, HIDDEN], F32R)
        w2_lo = sb("w2_lo", [P, EXPERTS, HIDDEN], F32R)
        w3_sb = sb("w3_sb", [P, EXPERTS, E])

        rows = sb("rows", [P, MP, FRAMES])
        emb = sb("emb", [P, BLOCKS, 2, E])
        hx = sb("hx", [P, TOKENS])
        squares = sb("squares", [P, TOKENS])
        stats = [[sb(f"stats{n}_{k}", [P, 2 * BLOCKS]) for k in range(5)] for n in range(2)]
        qkv = sb("qkv", [P, BLOCKS, 3 * P])
        kpart = sb("kpart", [P, 2, P])
        kmax = sb("kmax", [P, 1])
        kdiag = sb("kdiag", [P, P])
        qmax = sb("qmax", [P, BLOCKS, 2 * E // HEAD])
        qsum = sb("qsum", [P, BLOCKS, 2 * E // HEAD])
        qinv = sb("qinv", [P, BLOCKS, 2 * E // HEAD])
        ksum = sb("ksum", [P, TILES, P])
        ctxT = sb("ctxT", [P, P])
        kinv = sb("kinv", [P, 1])
        mix = sb("mix", [P, P])
        qsT = sb("qsT", [P, TOKENS])
        h2 = sb("h2", [P, BLOCKS, 2, E])
        z = sb("z", [P, BLOCKS, 2, E])

        zs = [sb(f"zs{n}", [P, CHUNK], F32R) for n in range(CHUNKS)]
        residual = [sb(f"residual{n}", [P, TILES, E]) for n in range(CHUNKS)]
        logits_lo = sb("logits_lo", [P, TILES, EXPERTS])
        logits = sb("logits", [P, TILES, EXPERTS])
        top = sb("top", [P, TILES, 8])
        top_id = sb("top_id", [P, TILES, 8], U32)
        margin = sb("margin", [P, TILES])
        half_tanh = sb("half_tanh", [P, TILES])
        share = [sb(f"share{n}", [P, TILES]) for n in range(2)]
        hot = [sb(f"hot{n}", [P, TILES, EXPERTS]) for n in range(2)]
        weighted = [sb(f"weighted{n}", [P, TILES, EXPERTS]) for n in range(2)]
        gates = sb("gates", [P, TILES, EXPERTS])
        gatesT = sb("gatesT", [TILES * EXPERTS, P])
        gate_rows = [sb(f"gate_rows{n}", [P, EPAIRS, CHUNK]) for n in range(2)]
        silu = [sb(f"silu{n}", [P, CHUNK]) for n in range(SILUS)]
        hid = [sb(f"hid{n}", [P, CHUNK]) for n in range(HIDS)]
        gated = [sb(f"gated{n}", [P, CHUNK]) for n in range(GATED)]
        acc = [sb(f"acc{n}", [P, CHUNK]) for n in range(2)]
        result = [sb(f"result{n}", [P, TILES, E]) for n in range(2)]

        h1_ps = [bank(f"h1_ps{n}") for n in range(2)]
        h2_ps = [bank(f"h2_ps{n}") for n in range(2)]
        y_ps = bank("y_ps")
        tail_ps = bank("tail_ps")
        att_ps = [bank(f"att_ps{n}") for n in range(2)]

        passed = sem("passed")
        tok_w_loaded = sem("tok_w_loaded")
        embed_in = sem("embed_in")
        small_in = sem("small_in")
        experts_in = sem("experts_in")
        pool_const = sem("pool_const")
        setup_perm = sem("setup_perm")
        setup_turned = sem("setup_turned")
        setup_zero = sem("setup_zero")
        setup_done = sem("setup_done")
        positions_ready = sem("positions_ready")
        split_hi = sem("split_hi")
        experts_hi = sem("experts_hi")
        experts_ready = sem("experts_ready")
        rows_in = sem("rows_in")
        emb_ps_ready = sem("emb_ps_ready")
        emb_ready = sem("emb_ready")
        emb_stored = sem("emb_stored")
        hx_in = sem("hx_in")
        bias_added = sem("bias_added")
        sum_done = [sem(f"sum_done{n}") for n in range(2)]
        mean_ready = [sem(f"mean_ready{n}") for n in range(2)]
        centered = [sem(f"centered{n}") for n in range(2)]
        squared = [sem(f"squared{n}") for n in range(2)]
        sq_sum_done = [sem(f"sq_sum_done{n}") for n in range(2)]
        var_ready = [sem(f"var_ready{n}") for n in range(2)]
        rstd_ready = [sem(f"rstd_ready{n}") for n in range(2)]
        normed = [sem(f"normed{n}") for n in range(2)]
        qkv_ps_ready = sem("qkv_ps_ready")
        qkv_copied = sem("qkv_copied")
        qkv_even = sem("qkv_even")
        qkv_odd = sem("qkv_odd")
        kpart_ready = sem("kpart_ready")
        kpart_turned = sem("kpart_turned")
        kmax_ready = sem("kmax_ready")
        kdiag_ready = sem("kdiag_ready")
        kmax_spread = sem("kmax_spread")
        k_shifted = sem("k_shifted")
        k_exp = sem("k_exp")
        qmax_ready = sem("qmax_ready")
        q_shifted = sem("q_shifted")
        q_exp = sem("q_exp")
        qsum_ready = sem("qsum_ready")
        qinv_ready = sem("qinv_ready")
        q_ready = sem("q_ready")
        ksum_ready = sem("ksum_ready")
        ctx_ps_ready = sem("ctx_ps_ready")
        ctx_ready = sem("ctx_ready")
        mix_ps_ready = sem("mix_ps_ready")
        kinv_ready = sem("kinv_ready")
        mix_ready = sem("mix_ready")
        q_turned = sem("q_turned")
        qsT_ready = sem("qsT_ready")
        attended = sem("attended")
        h2_ready = sem("h2_ready")
        z_turned = sem("z_turned")
        z_hi = sem("z_hi")
        residual_kept = sem("residual_kept")
        z_split = sem("z_split")
        logits_ps_ready = sem("logits_ps_ready")
        logits_lo_ready = sem("logits_lo_ready")
        logits_ready = sem("logits_ready")
        top_ready = sem("top_ready")
        top_id_ready = sem("top_id_ready")
        margin_ready = sem("margin_ready")
        tanh_ready = sem("tanh_ready")
        shares_ready = sem("shares_ready")
        hot_ready = sem("hot_ready")
        weighted_ready = sem("weighted_ready")
        gates_ready = sem("gates_ready")
        gates_turned = sem("gates_turned")
        gatesT_ready = sem("gatesT_ready")
        gates_stored = sem("gates_stored")
        early_rows_in = [sem(f"early_rows_in{n}") for n in range(2)]
        gate_rows_in = [sem(f"gate_rows_in{n}") for n in range(2)]
        h1_done = sem("h1_done")
        h2_done = sem("h2_done")
        silu_done = sem("silu_done")
        hid_done = sem("hid_done")
        y_done = sem("y_done")
        gated_done = sem("gated_done")
        acc_done = sem("acc_done")
        folded = sem("folded")
        result_ready = sem("result_ready")
        result_out = [sem(f"result_out{n}") for n in range(2)]

        EMBED_DMAS = 1 + 1
        SMALL_DMAS = 8 + 1 + 6 + 2 + 1
        block = ctx.enter_context(nc.Block())

        def reuse(eng, last_use, count):
            if not isinstance(count, int) or count > 0:
                eng.wait_ge(last_use, count)

        def lone_wait(eng, signal, count):
            eng.wait_ge(signal, count)
            eng.sem_inc(passed, 1)

        def before(m, c):
            return (m, c - 1) if c else (m - 1, CHUNKS - 1)

        def projected(m, k):
            c, e = divmod(k, EXPERTS)
            if e % 2 == 0:
                return None
            if e >= 3:
                return m, c, (e - 3) // 2
            started = c > 0 or not isinstance(m, int) or m > 0
            return (*before(m, c), EPAIRS - 1) if started else None

        def place(c):
            t0 = c % (CHUNKS // 2) * TILES
            return c // (CHUNKS // 2), slice(t0, t0 + TILES)

        def split(m, c):
            return CHUNKS * m + (1, 3, 2, 4)[c]

        def uses(m, c):
            return CHUNKS // 2 * m + c // 2 + 1

        def for_slots(eng, attend, experts):
            for k in range(SLOTS):
                attend(0, k)
            for k in range(SLOTS):
                experts(0, k)
                attend(1, k)
            with eng.Fori(1, PAIRS - 1) as m:
                for k in range(SLOTS):
                    experts(m, k)
                    attend(m + 1, k)
            for k in range(SLOTS):
                experts(PAIRS - 1, k)

        def for_routes(m, k, route):
            for c in range(1, CHUNKS):
                if ROUTE[c] <= k < ROUTE[c] + EXPERTS:
                    route(m, c, k - ROUTE[c])

        @block.sync
        def _(sp):
            def load_rows(m):
                for b in range(2):
                    for i in range(PATCH):
                        row = x[2 * m + b, 0, i, :]
                        src = bass.AP(tensor=row.tensor, offset=row.offset,
                                      ap=[[1, PATCH], [PATCH * FRAMES, MP], [1, SHIFTED]])
                        p0 = b * E + i * PATCH
                        sp.dma_start(rows[p0:p0 + PATCH, :, 0:SHIFTED], src).then_inc(rows_in, 16)

            def spread_gates(m, c):
                n, ring = CHUNKS * m + c, c % 2
                lone_wait(sp, gatesT_ready, n + 1)
                sp.dma_start(gates_dram[ring].rearrange("e (t s) -> t e s", s=P),
                             gatesT[:, :]).then_inc(gates_stored, 16)
                lone_wait(sp, gates_stored, 16 * (n + 1))
                if not isinstance(n, int) or n > 1:
                    lone_wait(sp, gated_done, EPAIRS * (n - 1))
                for qs, rows_loaded in ((slice(0, EARLY), early_rows_in), (slice(EARLY, EPAIRS), gate_rows_in)):
                    for half in range(2):
                        src = gates_dram[ring].rearrange("(q a) t -> a q t", a=2)[half, qs]
                        sp.dma_start(gate_rows[ring][half * E:(half + 1) * E, qs, :],
                                     src.partition_broadcast(E)).then_inc(rows_loaded[ring], 16)

            def store(m, c):
                b, blocks = place(c)
                lone_wait(sp, result_ready, CHUNKS * m + c + 1)
                dst = out[2 * m + b, blocks.start * P:blocks.stop * P, :].rearrange("(t s) e -> s t e", s=P)
                sp.dma_start(dst, result[c % 2][:, :, :]).then_inc(result_out[c % 2], 16)

            def store_embedding(m):
                if not isinstance(m, int) or m > 0:
                    lone_wait(sp, attended, 2 * m)
                for u in range(2):
                    lone_wait(sp, emb_ready, 4 * m + 2 * u + 2)
                    for b in range(2):
                        dst = embed_dram[b, u * CHUNK:(u + 1) * CHUNK, :].rearrange("(t s) e -> s t e", s=P)
                        sp.dma_start(dst, emb[:, u * TILES:(u + 1) * TILES, b, :]).then_inc(emb_stored, 16)

            def load_channels(m):
                lone_wait(sp, emb_stored, 64 * (m + 1))
                for b in range(2):
                    sp.dma_start(hx[b * E:(b + 1) * E, :],
                                 embed_dram[b].rearrange("(c r) e -> c (r e)", r=ROWS)).then_inc(hx_in, 16)

            def pair(m, first, rows_left, pairs_left):
                if pairs_left:
                    store_embedding(m + 1)
                    load_channels(m + 1)
                if not first:
                    store(m - 1, 3)
                spread_gates(m, 1)
                if rows_left:
                    load_rows(m + 2)
                store(m, 0)
                spread_gates(m, 2)
                store(m, 1)
                spread_gates(m, 3)
                if pairs_left:
                    spread_gates(m + 1, 0)
                store(m, 2)

            def small(dst, src, loaded=small_in):
                sp.dma_start(dst, src).then_inc(loaded, 16)

            for d in range(2):
                small(tok_w_in[:, d, :], tok_w, tok_w_loaded)
            load_rows(0)
            small(emb_bias[:, :], tok_b.partition_broadcast(P), embed_in)
            small(pos_tok[:, :, :], pos[0].rearrange("(t s) e -> s t e", s=P), embed_in)
            for n, w in enumerate((wq, wk, wv, wr)):
                for d in range(2):
                    small(proj_in[:, n, d, :], w)
            store_embedding(0)
            for n, bias in enumerate((bq, bk, bv)):
                for d in range(2):
                    small(qkv_bias[:, n, d, :], bias.partition_broadcast(P))
            small(out_bias[:, :], br.partition_broadcast(P))
            load_channels(0)
            for d in range(2):
                small(gate_in[d * E:(d + 1) * E, :], gate_w)
            small(gate_bias[:, :], gate_b.partition_broadcast(P))
            for ring, w in enumerate((w1, w2)):
                for d in range(2):
                    raw = gate_rows[ring][d * E:(d + 1) * E, 0:4, :].rearrange("p a (b h) -> p (a b) h", h=HIDDEN)
                    sp.dma_start(raw, w.rearrange("e d h -> d e h")).then_inc(experts_in, 16)
            sp.dma_start(w3_sb[:, :, :], w3.rearrange("e h d -> h e d")).then_inc(experts_in, 16)
            load_rows(1)
            sp.wait_ge(experts_ready, 2)
            spread_gates(0, 0)
            pair(0, True, True, True)
            with sp.Fori(1, PAIRS - 2) as m:
                pair(m, False, True, True)
            pair(PAIRS - 2, False, False, True)
            pair(PAIRS - 1, False, False, False)
            store(PAIRS - 1, 3)
            for n in range(2):
                sp.wait_ge(result_out[n], 16 * PAIRS * CHUNKS // 2)

        @block.gpsimd
        def _(pool):
            gp = nc.gpsimd
            gp.memset(ident[:, :], 0.0).then_inc(pool_const, 1)
            gp.memset(fold[:, :], 0.0).then_inc(pool_const, 1)
            gp.memset(head_mask[:, :], 1.0).then_inc(pool_const, 1)
            gp.memset(ones[:, :], 1.0).then_inc(pool_const, 1)
            gp.memset(minus_half[:, :], -0.5).then_inc(pool_const, 1)
            gp.iota(expert_id[:, :], [[1, EXPERTS]], base=0, channel_multiplier=0,
                    allow_small_or_imprecise_dtypes=True).then_inc(pool_const, 1)
            pool.wait_ge(pool_const, 6)
            gp.affine_select(out=ident[:, :], in_=ident[:, :], compare_op=ALU.not_equal, fill=1.0,
                             base=0, pattern=[[-1, P]], channel_multiplier=1).then_inc(pool_const, 1)
            gp.affine_select(out=fold[:, :], in_=fold[:, :], compare_op=ALU.not_equal, fill=1.0,
                             base=0, pattern=[[-1, E]], channel_multiplier=1).then_inc(pool_const, 1)
            hm = head_mask[:, :].rearrange("p (g j) -> p g j", j=HEAD)
            gp.affine_select(out=hm, in_=hm, compare_op=ALU.is_ge, fill=0.0,
                             base=0, pattern=[[-HEAD, P // HEAD], [0, HEAD]], channel_multiplier=1).then_inc(pool_const, 1)
            pool.wait_ge(pool_const, 9)
            gp.affine_select(out=fold[:, :], in_=fold[:, :], compare_op=ALU.not_equal, fill=1.0,
                             base=-E, pattern=[[-1, E]], channel_multiplier=1).then_inc(pool_const, 1)
            gp.affine_select(out=hm, in_=hm, compare_op=ALU.is_ge, fill=0.0,
                             base=HEAD - 1, pattern=[[HEAD, P // HEAD], [0, HEAD]], channel_multiplier=-1).then_inc(pool_const, 1)

            hx_groups = hx[:, :].rearrange("p (g e) -> p g e", e=E)
            emb_groups = emb[:, :, :, :].rearrange("p t b e -> p (t b) e")
            h2_groups = h2[:, :, :, :].rearrange("p t b e -> p (t b) e")
            z_groups = z[:, :, :, :].rearrange("p t b e -> p (t b) e")
            q_heads = qkv[:, :, 0:P].rearrange("p t (g j) -> p t g j", j=HEAD)

            def norm_center(ln, m, u, dst, src):
                half = slice(u * BLOCKS, (u + 1) * BLOCKS)
                pool.wait_ge(mean_ready[ln], 2 * m + u + 1)
                mean = stats[ln][1][:, half].unsqueeze(2).broadcast_to([P, BLOCKS, E])
                gp.tensor_tensor(dst[:, half], src[:, half], mean, ALU.subtract).then_inc(centered[ln], 1)

            def norm_scale(ln, m, u, data):
                half = slice(u * BLOCKS, (u + 1) * BLOCKS)
                pool.wait_ge(var_ready[ln], 2 * m + u + 1)
                gp.tensor_tensor(stats[ln][4][:, half], stats[ln][3][:, half], minus_half[:, :],
                                 ALU.pow).then_inc(rstd_ready[ln], 1)
                pool.wait_ge(rstd_ready[ln], 2 * m + u + 1)
                rstd = stats[ln][4][:, half].unsqueeze(2).broadcast_to([P, BLOCKS, E])
                gp.tensor_tensor(data[:, half], data[:, half], rstd, ALU.mult).then_inc(normed[ln], 1)

            def attend(m, k):
                if k in CENTER1:
                    norm_center(0, m, CENTER1.index(k), hx_groups, hx_groups)
                if k in ADD_BIAS:
                    u = ADD_BIAS.index(k)
                    half = slice(u * BLOCKS, (u + 1) * BLOCKS)
                    if isinstance(m, int) and m == 0:
                        pool.wait_ge(small_in, 16 * SMALL_DMAS)
                    pool.wait_ge(emb_stored, 64 * (m + 1))
                    gp.tensor_tensor(emb_groups[:, half], emb_groups[:, half],
                                     out_bias[:, :].unsqueeze(1).broadcast_to([P, BLOCKS, E]), ALU.add).then_inc(bias_added, 1)
                if k in SCALE1:
                    norm_scale(0, m, SCALE1.index(k), hx_groups)
                if k in QKV_OUT and QKV_OUT.index(k) % 2 == 0:
                    t = QKV_OUT.index(k)
                    if isinstance(m, int) and m == 0 and t == 0:
                        pool.wait_ge(small_in, 16 * SMALL_DMAS)
                    pool.wait_ge(qkv_copied, BLOCKS // 2 * m + t // 2 + 1)
                    gp.tensor_tensor(qkv[:, t, :], qkv[:, t, :], qkv_bias[:, :, :, :].rearrange("p n d e -> p (n d e)"),
                                     ALU.add).then_inc(qkv_even, 1)
                for slots, signal, per_head, done in ((QCENTER, qmax_ready, qmax, q_shifted), (QSCALE, qinv_ready, qinv, q_ready)):
                    if k in slots:
                        u = slots.index(k)
                        half = slice(u * TILES, (u + 1) * TILES)
                        pool.wait_ge(signal, 2 * m + u + 1)
                        gp.tensor_tensor(q_heads[:, half], q_heads[:, half],
                                         per_head[:, half, :].unsqueeze(3).broadcast_to([P, TILES, P // HEAD, HEAD]),
                                         ALU.subtract if slots is QCENTER else ALU.mult).then_inc(done, 1)
                if k == KSUM:
                    pool.wait_ge(k_exp, m + 1)
                    reuse(pool, mix_ps_ready, m)
                    gp.tensor_tensor(ksum[:, :, :], qkv[:, 0:TILES, P:2 * P], qkv[:, TILES:BLOCKS, P:2 * P],
                                     ALU.add).then_inc(ksum_ready, 1)
                    pool.wait_ge(ksum_ready, 3 * m + 1)
                    gp.tensor_tensor(ksum[:, 0:2, :], ksum[:, 0:2, :], ksum[:, 2:4, :], ALU.add).then_inc(ksum_ready, 1)
                    pool.wait_ge(ksum_ready, 3 * m + 2)
                    gp.tensor_tensor(ksum[:, 0, :], ksum[:, 0, :], ksum[:, 1, :], ALU.add).then_inc(ksum_ready, 1)
                if k in CENTER2:
                    reuse(pool, z_turned, 2 * m)
                    norm_center(1, m, CENTER2.index(k), z_groups, h2_groups)
                if k in SCALE2:
                    norm_scale(1, m, SCALE2.index(k), z_groups)

            def accumulate(m, c, q):
                n = CHUNKS * m + c
                pool.wait_ge(gated_done, EPAIRS * n + q + 1)
                if q > 1:
                    pool.wait_ge(acc_done, (EPAIRS - 1) * n + q - 1)
                gp.tensor_tensor(acc[c % 2][:, :], acc[c % 2][:, :], gated[q % GATED][:, :],
                                 ALU.add).then_inc(acc_done, 1)

            def experts(m, k):
                at = projected(m, k)
                if at and at[2] > 0:
                    accumulate(*at)

            for_slots(pool, attend, experts)
            accumulate(PAIRS - 1, CHUNKS - 1, EPAIRS - 1)

        @block.scalar
        def _(act):
            sc = nc.scalar

            def route(m, c, step):
                n = CHUNKS * m + c
                b, blocks = place(c)
                if step == Z_HI:
                    if c < CHUNKS // 2:
                        act.wait_ge(z_turned, 2 * m + c + 1)
                        for i in range(2):
                            reuse(act, h2_done, EXPERTS * (n + 2 * i - CHUNKS + 1) if not isinstance(m, int) or m > 0 else 0)
                            img = slice(i * E, (i + 1) * E)
                            sc.activation(zs[c + 2 * i][img, :], tail_ps[img, :], ACT.Copy).then_inc(z_hi, 1)
                    reuse(act, result_ready, n - CHUNKS + 1)
                    sc.activation(residual[c][:, :, :], h2[:, blocks, b, :], ACT.Copy).then_inc(residual_kept, 1)
                if step == SHARES:
                    act.wait_ge(margin_ready, n + 1)
                    reuse(act, shares_ready, 2 * n)
                    sc.activation(half_tanh[:, :], margin[:, :], ACT.Tanh, scale=0.5).then_inc(tanh_ready, 1)
                if step == GATES_OUT:
                    act.wait_ge(gates_turned, n + 1)
                    reuse(act, gates_stored, 16 * n)
                    sc.activation(gatesT[:, :], tail_ps[0:TILES * EXPERTS, 0:P], ACT.Copy).then_inc(gatesT_ready, 1)

            def attend(m, k):
                if k in SQUARE1:
                    u = SQUARE1.index(k)
                    half = slice(u * CHUNK, (u + 1) * CHUNK)
                    act.wait_ge(centered[0], 2 * m + u + 1)
                    reuse(act, sq_sum_done[1], 2 * (m - 1) + u + 1 if not isinstance(m, int) or m > 0 else 0)
                    sc.activation(squares[:, half], hx[:, half], ACT.Square).then_inc(squared[0], 1)
                if k in QKV_OUT and QKV_OUT.index(k) % 2 == 0:
                    t = QKV_OUT.index(k)
                    act.wait_ge(qkv_ps_ready, BLOCKS * m + t + 1)
                    reuse(act, q_turned, 2 * m)
                    sc.activation(qkv[:, t, :], att_ps[0][:, 0:3 * P], ACT.Copy).then_inc(qkv_copied, 1)
                if k == EXPS:
                    act.wait_ge(k_shifted, 2 * m + 2)
                    sc.activation(qkv[:, :, P:2 * P], qkv[:, :, P:2 * P], ACT.Exp).then_inc(k_exp, 1)
                    act.wait_ge(q_shifted, 2 * m + 2)
                    sc.activation(qkv[:, :, 0:P], qkv[:, :, 0:P], ACT.Exp).then_inc(q_exp, 1)
                if k in QTURN:
                    u = QTURN.index(k)
                    act.wait_ge(q_turned, 2 * m + u + 1)
                    reuse(act, attended, 2 * m)
                    sc.activation(qsT[:, u * CHUNK:(u + 1) * CHUNK], att_ps[u][:, :], ACT.Copy).then_inc(qsT_ready, 1)
                if k in SQUARE2:
                    u = SQUARE2.index(k)
                    act.wait_ge(centered[1], 2 * m + u + 1)
                    sc.activation(squares[:, u * CHUNK:(u + 1) * CHUNK],
                                  z[:, u * TILES:(u + 1) * TILES, :, :].rearrange("p t b e -> p (t b e)"),
                                  ACT.Square).then_inc(squared[1], 1)
                if k >= ROUTE[0]:
                    route(m, 0, k - ROUTE[0])

            def experts(m, k):
                g = SLOTS * m + k
                act.wait_ge(h1_done, g + 1)
                reuse(act, hid_done, g - SILUS + 1)
                sc.activation(silu[k % SILUS][:, :], h1_ps[k % 2][:, :], ACT.Silu).then_inc(silu_done, 1)
                for_routes(m, k, route)

            def attend_first(m, k):
                if isinstance(m, int) and m == 0 and k == KMAX:
                    act.wait_ge(experts_in, 16 * 5)
                    for raw, hi in zip(gate_rows, (w1_hi, w2_hi)):
                        sc.activation(hi[:, :, :], raw[:, 0:4, :].rearrange("p a (b h) -> p (a b) h", h=HIDDEN),
                                      ACT.Copy).then_inc(experts_hi, 1)
                attend(m, k)

            for_slots(act, attend_first, experts)

        @block.vector
        def _(dve):
            ve = nc.vector
            hx_groups = hx[:, :].rearrange("p (g e) -> p g e", e=E)
            h2_groups = h2[:, :, :, :].rearrange("p t b e -> p (t b) e")
            q_heads = qkv[:, :, 0:P].rearrange("p t (g j) -> p t g j", j=HEAD)
            keys = qkv[:, :, P:2 * P]

            ve.memset(proj[:, :, :], 0.0).then_inc(setup_zero, 1)
            ve.memset(tok_w_both[:, :], 0.0).then_inc(setup_zero, 1)
            dve.wait_ge(tok_w_loaded, 16 * 2)
            ve.tensor_copy(tok_w_perm[:, :], tok_w_in[:, :, :].rearrange("e d k -> e (d k)")).then_inc(setup_perm, 1)
            dve.wait_ge(setup_turned, 1)
            dve.wait_ge(setup_zero, 2)
            for d in range(2):
                ve.tensor_copy(tok_w_both[d * E:(d + 1) * E, d * E:(d + 1) * E],
                               att_ps[0][d * E:(d + 1) * E, 0:E]).then_inc(setup_done, 1)

            dve.wait_ge(embed_in, 16 * EMBED_DMAS)
            ve.tensor_tensor(pos_tok[:, :, :], pos_tok[:, :, :],
                             emb_bias[:, :].unsqueeze(1).broadcast_to([P, BLOCKS, E]), ALU.add).then_inc(positions_ready, 1)

            def setup_rest():
                dve.wait_ge(small_in, 16 * SMALL_DMAS)
                ve.tensor_copy(gate_split[:, 0, :], gate_in[:, :]).then_inc(split_hi, 1)
                dve.wait_ge(split_hi, 1)
                ve.tensor_tensor(gate_split[:, 1, :], gate_in[:, :], gate_split[:, 0, :].bitcast(F32), ALU.subtract).then_inc(setup_done, 1)
                dve.wait_ge(setup_turned, 2)
                turned = tail_ps[:, 0:4 * E].rearrange("p (n e) -> p n e", n=4)
                for d in range(2):
                    ve.tensor_copy(proj[d * E:(d + 1) * E, :, d * E:(d + 1) * E],
                                   turned[d * E:(d + 1) * E]).then_inc(setup_done, 1)

            def split_low(n):
                hi, lo = ((w1_hi, w1_lo), (w2_hi, w2_lo))[n]
                dve.wait_ge(experts_in, 16 * 5)
                dve.wait_ge(experts_hi, n + 1)
                raw = gate_rows[n][:, 0:4, :].rearrange("p a (b h) -> p (a b) h", h=HIDDEN)
                ve.tensor_tensor(lo[:, :, :], raw, hi[:, :, :].bitcast(F32), ALU.subtract).then_inc(experts_ready, 1)

            def norm_sum(ln, m, u, data):
                half = slice(u * BLOCKS, (u + 1) * BLOCKS)
                ve.tensor_reduce(stats[ln][0][:, half], data[:, half], AX_X, ALU.add).then_inc(sum_done[ln], 1)
                dve.wait_ge(sum_done[ln], 2 * m + u + 1)
                ve.tensor_scalar(stats[ln][1][:, half], stats[ln][0][:, half], 1.0 / E, None, ALU.mult).then_inc(mean_ready[ln], 1)

            def norm_var(ln, m, u):
                half = slice(u * BLOCKS, (u + 1) * BLOCKS)
                dve.wait_ge(squared[ln], 2 * m + u + 1)
                ve.tensor_reduce(stats[ln][2][:, half], squares[:, u * CHUNK:(u + 1) * CHUNK].rearrange("p (g e) -> p g e", e=E),
                                 AX_X, ALU.add).then_inc(sq_sum_done[ln], 1)
                dve.wait_ge(sq_sum_done[ln], 2 * m + u + 1)
                ve.tensor_scalar(stats[ln][3][:, half], stats[ln][2][:, half], 1.0 / E, EPS,
                                 ALU.mult, ALU.add).then_inc(var_ready[ln], 1)

            def wait_qkv(m, u):
                dve.wait_ge(qkv_even, BLOCKS // 2 * m + TILES // 2 * (u + 1))
                dve.wait_ge(qkv_odd, BLOCKS // 2 * m + TILES // 2 * (u + 1))

            def attend(m, k):
                if k in ADD1:
                    u = ADD1.index(k)
                    dve.wait_ge(emb_ps_ready, 2 * m + u + 1)
                    reuse(dve, h2_ready, 4 * m)
                    if isinstance(m, int) and m == 0:
                        dve.wait_ge(positions_ready, 1)
                    half = slice(u * TILES, (u + 1) * TILES)
                    for b in range(2):
                        ve.tensor_tensor(emb[:, half, b, :],
                                         att_ps[u][:, :].rearrange("p (t b e) -> p t b e", t=TILES, b=2)[:, :, b, :],
                                         pos_tok[:, half, :], ALU.add).then_inc(emb_ready, 1)
                if k in MEAN1:
                    dve.wait_ge(hx_in, 32 * (m + 1))
                    norm_sum(0, m, MEAN1.index(k), hx_groups)
                if k in VAR1:
                    norm_var(0, m, VAR1.index(k))
                if k in QKV_OUT and QKV_OUT.index(k) % 2 == 1:
                    t = QKV_OUT.index(k)
                    dve.wait_ge(qkv_ps_ready, BLOCKS * m + t + 1)
                    reuse(dve, q_turned, 2 * m)
                    ve.tensor_tensor(qkv[:, t, :], att_ps[1][:, 0:3 * P], qkv_bias[:, :, :, :].rearrange("p n d e -> p (n d e)"),
                                     ALU.add).then_inc(qkv_odd, 1)
                if k in KPART:
                    u = KPART.index(k)
                    wait_qkv(m, u)
                    ve.tensor_reduce(kpart[:, u, :], keys[:, u * TILES:(u + 1) * TILES].rearrange("p t c -> p c t"),
                                     AX_X, ALU.max).then_inc(kpart_ready, 1)
                if k in QMAX:
                    u = QMAX.index(k)
                    half = slice(u * TILES, (u + 1) * TILES)
                    wait_qkv(m, u)
                    ve.tensor_reduce(qmax[:, half, :], q_heads[:, half], AX_X, ALU.max).then_inc(qmax_ready, 1)
                if k == KMAX:
                    dve.wait_ge(kpart_turned, m + 1)
                    ve.tensor_reduce(kmax[:, :], att_ps[0][:, 0:2 * P], AX_X, ALU.max).then_inc(kmax_ready, 1)
                    dve.wait_ge(kmax_ready, m + 1)
                    ve.tensor_scalar(kdiag[:, :], ident[:, :], kmax[:, 0:1], None, ALU.mult).then_inc(kdiag_ready, 1)
                if k in KSUB:
                    u = KSUB.index(k)
                    half = keys[:, u * TILES:(u + 1) * TILES]
                    dve.wait_ge(kmax_spread, m + 1)
                    ve.tensor_tensor(half, half, att_ps[1][:, 0:P].unsqueeze(1).broadcast_to([P, TILES, P]),
                                     ALU.subtract).then_inc(k_shifted, 1)
                if k in QSUM:
                    u = QSUM.index(k)
                    half = slice(u * TILES, (u + 1) * TILES)
                    dve.wait_ge(q_exp, m + 1)
                    ve.tensor_reduce(qsum[:, half, :], q_heads[:, half], AX_X, ALU.add).then_inc(qsum_ready, 1)
                    dve.wait_ge(qsum_ready, 2 * m + u + 1)
                    ve.reciprocal(qinv[:, half, :], qsum[:, half, :]).then_inc(qinv_ready, 1)
                if k == CMASK:
                    dve.wait_ge(ctx_ps_ready, m + 1)
                    ve.tensor_tensor(ctxT[:, :], att_ps[0][:, 0:P], head_mask[:, :], ALU.mult).then_inc(ctx_ready, 1)
                if k == MSCALE:
                    dve.wait_ge(mix_ps_ready, m + 1)
                    ve.reciprocal(kinv[:, :], att_ps[1][:, P:P + 1]).then_inc(kinv_ready, 1)
                    dve.wait_ge(kinv_ready, m + 1)
                    ve.tensor_scalar(mix[:, :], att_ps[1][:, 0:P], kinv[:, 0:1], None, ALU.mult).then_inc(mix_ready, 1)
                if k in ADD2:
                    u = ADD2.index(k)
                    dve.wait_ge(attended, 2 * m + u + 1)
                    dve.wait_ge(bias_added, 2 * m + u + 1)
                    reuse(dve, residual_kept, CHUNKS * m)
                    half = slice(u * TILES, (u + 1) * TILES)
                    for b in range(2):
                        ve.tensor_tensor(h2[:, half, b, :],
                                         att_ps[u][:, :].rearrange("p (t b e) -> p t b e", t=TILES, b=2)[:, :, b, :],
                                         emb[:, half, b, :], ALU.add).then_inc(h2_ready, 1)
                if k in MEAN2:
                    dve.wait_ge(h2_ready, 4 * m + 2 * MEAN2.index(k) + 2)
                    norm_sum(1, m, MEAN2.index(k), h2_groups)
                if k in VAR2:
                    norm_var(1, m, VAR2.index(k))
                if k >= ROUTE[0]:
                    route(m, 0, k - ROUTE[0])

            def route(m, c, step):
                n = CHUNKS * m + c
                if step in (Z_LO, Z_LO + 1) and c < CHUNKS // 2:
                    i = step - Z_LO
                    img, other = slice(i * E, (i + 1) * E), slice((1 - i) * E, (2 - i) * E)
                    dve.wait_ge(z_hi, CHUNKS * m + 2 * c + i + 1)
                    ve.tensor_tensor(zs[c + 2 * i][other, :], tail_ps[img, :], zs[c + 2 * i][img, :].bitcast(F32),
                                     ALU.subtract).then_inc(z_split, 1)
                if step == LOGITS_OUT:
                    dve.wait_ge(logits_ps_ready, n + 1)
                    parts = tail_ps[:, 0:TILES * 2 * EXPERTS].rearrange("p (t h e) -> p t h e", h=2, e=EXPERTS)
                    ve.tensor_tensor(logits_lo[:, :, :], parts[:, :, 1, :],
                                     gate_bias[:, :].unsqueeze(1).broadcast_to([P, TILES, EXPERTS]),
                                     ALU.add).then_inc(logits_lo_ready, 1)
                    dve.wait_ge(logits_lo_ready, n + 1)
                    ve.tensor_tensor(logits[:, :, :], parts[:, :, 0, :], logits_lo[:, :, :], ALU.add).then_inc(logits_ready, 1)
                if step == TOP:
                    lone_wait(dve, logits_ready, n + 1)
                    for j in range(TILES):
                        ve.max(top[:, j, :], logits[:, j, :]).then_inc(top_ready, 1)
                    dve.wait_ge(top_ready, TILES * (n + 1))
                    reuse(dve, tanh_ready, n)
                    ve.tensor_tensor(margin[:, :], top[:, :, 0], top[:, :, 1], ALU.subtract).then_inc(margin_ready, 1)
                    for j in range(TILES):
                        ve.max_index(top_id[:, j, :], top[:, j, :], logits[:, j, :]).then_inc(top_id_ready, 1)
                if step == SHARES:
                    dve.wait_ge(top_id_ready, TILES * (n + 1))
                    for r in range(2):
                        ve.tensor_tensor(hot[r][:, :, :], expert_id[:, :].unsqueeze(1).broadcast_to([P, TILES, EXPERTS]),
                                         top_id[:, :, r].unsqueeze(2).broadcast_to([P, TILES, EXPERTS]),
                                         ALU.is_equal).then_inc(hot_ready, 1)
                    dve.wait_ge(tanh_ready, n + 1)
                    for r in range(2):
                        ve.tensor_scalar(share[r][:, :], half_tanh[:, :], 0.5 - r, 0.5, ALU.mult, ALU.add).then_inc(shares_ready, 1)
                if step == GATES:
                    dve.wait_ge(hot_ready, 2 * (n + 1))
                    dve.wait_ge(shares_ready, 2 * (n + 1))
                    for r in range(2):
                        ve.tensor_tensor(weighted[r][:, :, :], hot[r][:, :, :],
                                         share[r][:, :].unsqueeze(2).broadcast_to([P, TILES, EXPERTS]),
                                         ALU.mult).then_inc(weighted_ready, 1)
                    dve.wait_ge(weighted_ready, 2 * (n + 1))
                    reuse(dve, gates_turned, n)
                    ve.tensor_tensor(gates[:, :, :], weighted[0][:, :, :], weighted[1][:, :, :],
                                     ALU.add).then_inc(gates_ready, 1)

            def weigh(m, c, q):
                n = CHUNKS * m + c
                others = EPAIRS - 1
                dve.wait_ge(y_done, EPAIRS * n + q + 1)
                if q in (0, EARLY):
                    dve.wait_ge((gate_rows_in if q else early_rows_in)[c % 2], 32 * uses(m, c))
                if q == 0:
                    reuse(dve, folded, n - 1)
                    dst = acc[c % 2]
                else:
                    reuse(dve, acc_done, others * n + q - GATED if q > GATED else others * (n - 1) + min(q + GATED, q % GATED + 4))
                    dst = gated[q % GATED]
                ve.tensor_tensor(dst[:, :], y_ps[:, :], gate_rows[c % 2][:, q, :], ALU.mult).then_inc(gated_done, 1)

            def finish(m, c):
                dve.wait_ge(folded, CHUNKS * m + c + 1)
                reuse(dve, result_out[c % 2], 16 * (uses(m, c) - 1))
                ve.tensor_tensor(result[c % 2][:, :, :], tail_ps[:, 0:TILES * E].rearrange("p (t e) -> p t e", e=E),
                                 residual[c][:, :, :], ALU.add).then_inc(result_ready, 1)

            def experts(m, k):
                c, e = divmod(k, EXPERTS)
                g = SLOTS * m + k
                started = c > 0 or not isinstance(m, int) or m > 0
                dve.wait_ge(silu_done, g + 1)
                dve.wait_ge(h2_done, g + 1)
                reuse(dve, y_done, SLOTS // 2 * m + (k - HIDS) // 2 + 1)
                ve.tensor_tensor(hid[k % HIDS][:, :], silu[k % SILUS][:, :], h2_ps[k % 2][:, :], ALU.mult).then_inc(hid_done, 1)
                if at := projected(m, k):
                    weigh(*at)
                if e == FINISH[c] and started:
                    finish(*before(m, c))
                for_routes(m, k, route)

            def attend_first(m, k):
                attend(m, k)
                if isinstance(m, int) and m == 0 and k == VAR1[0]:
                    setup_rest()
                if isinstance(m, int) and m == 0 and k in (KSUB[1], QTURN[1]):
                    split_low((KSUB[1], QTURN[1]).index(k))

            for_slots(dve, attend_first, experts)
            weigh(PAIRS - 1, CHUNKS - 1, EPAIRS - 1)
            finish(PAIRS - 1, CHUNKS - 1)

        @block.tensor
        def _(pe):
            te = nc.tensor
            samples = rows[:, :, :].rearrange("p m f -> p (m f)")
            pe.wait_ge(pool_const, 11)
            pe.wait_ge(setup_perm, 1)
            te.transpose(att_ps[0][:, 0:E], tok_w_perm[:, :], ident[0:E, 0:E]).then_inc(setup_turned, 1)
            pe.wait_ge(setup_done, 2)

            def setup_rest():
                pe.wait_ge(small_in, 16 * SMALL_DMAS)
                for n in range(4):
                    mm = te.transpose(tail_ps[:, n * E:(n + 1) * E], proj_in[:, n, :, :].rearrange("o d c -> o (d c)"),
                                      ident[0:E, 0:E])
                mm.then_inc(setup_turned, 1)
                pe.wait_ge(setup_done, 5)

            def attend(m, k):
                if k == EMBED:
                    reuse(pe, h2_ready, 4 * m)
                    lone_wait(pe, rows_in, 16 * 2 * PATCH * (m + 1))
                    for t in range(BLOCKS):
                        cols = samples[:, PATCH * P * t:PATCH * (P * (t + 1) - 1) + 1:PATCH]
                        mm = te.matmul(att_ps[t // TILES][:, t % TILES * P:(t % TILES + 1) * P], cols, tok_w_both[:, :],
                                       start=True, stop=True)
                        if t % TILES == TILES - 1:
                            mm.then_inc(emb_ps_ready, 1)
                if k in QKV:
                    t = QKV.index(k)
                    pe.wait_ge(normed[0], 2 * m + t // TILES + 1)
                    if t >= 2:
                        pe.wait_ge((qkv_copied, qkv_odd)[t % 2], BLOCKS // 2 * m + t // 2)
                    te.matmul(att_ps[t % 2][:, 0:3 * P], hx[:, t * P:(t + 1) * P],
                              proj[:, 0:3, :].rearrange("p n o -> p (n o)"), start=True, stop=True).then_inc(qkv_ps_ready, 1)
                if k == KTURN:
                    pe.wait_ge(kpart_ready, 2 * m + 2)
                    for u in range(2):
                        mm = te.transpose(att_ps[0][:, u * P:(u + 1) * P], kpart[:, u, :], ident[:, :])
                    mm.then_inc(kpart_turned, 1)
                if k == KSPREAD:
                    pe.wait_ge(kdiag_ready, m + 1)
                    te.matmul(att_ps[1][:, 0:P], ones[:, :], kdiag[:, :], start=True, stop=True).then_inc(kmax_spread, 1)
                if k == CONTEXT:
                    pe.wait_ge(k_exp, m + 1)
                    for t in range(BLOCKS):
                        mm = te.matmul(att_ps[0][:, 0:P], qkv[:, t, 2 * P:3 * P], qkv[:, t, P:2 * P],
                                       start=(t == 0), stop=(t == BLOCKS - 1))
                    mm.then_inc(ctx_ps_ready, 1)
                if k == MIX:
                    pe.wait_ge(ctx_ready, m + 1)
                    te.matmul(att_ps[1][:, 0:P], ctxT[:, :], proj[:, 3, :], start=True, stop=True)
                    pe.wait_ge(ksum_ready, 3 * (m + 1))
                    te.matmul(att_ps[1][:, P:P + 1], ksum[:, 0, :], ones[:, 0:1],
                              start=True, stop=True).then_inc(mix_ps_ready, 1)
                if k in QTURN:
                    u = QTURN.index(k)
                    pe.wait_ge(q_ready, 2 * m + u + 1)
                    pe.wait_ge(mix_ready, m + 1)
                    for j in range(TILES):
                        mm = te.transpose(att_ps[u][:, j * P:(j + 1) * P], qkv[:, u * TILES + j, 0:P], ident[:, :])
                    mm.then_inc(q_turned, 1)
                if k in ATTENDED:
                    u = ATTENDED.index(k)
                    pe.wait_ge(qsT_ready, 2 * m + u + 1)
                    for j in range(TILES):
                        t = u * TILES + j
                        o = att_ps[u][:, j * P:(j + 1) * P]
                        te.matmul(o, qsT[:, t * P:(t + 1) * P], mix[:, :], start=True, stop=False)
                        mm = te.matmul(o, hx[:, t * P:(t + 1) * P], ident[:, :], start=False, stop=True)
                    mm.then_inc(attended, 1)
                if k >= ROUTE[0]:
                    route(m, 0, k - ROUTE[0])

            def route(m, c, step):
                n = CHUNKS * m + c
                b, blocks = place(c)
                if step == Z_TURN and c < CHUNKS // 2:
                    if not isinstance(n, int) or n > 0:
                        pe.wait_ge(gatesT_ready, n)
                    if c == 1:
                        reuse(pe, result_ready, n - 2)
                    pe.wait_ge(normed[1], 2 * m + c + 1)
                    for j in range(TILES):
                        mm = te.transpose(tail_ps[:, j * P:(j + 1) * P], z[:, blocks.start + j, :, :].rearrange("p b e -> p (b e)"),
                                          ident[:, :])
                    mm.then_inc(z_turned, 1)
                if step == LOGITS:
                    pe.wait_ge(z_split, split(m, c + 2 if c < 2 else c))
                    if c >= CHUNKS // 2:
                        pe.wait_ge(gatesT_ready, n)
                    for j in range(TILES):
                        mm = te.matmul(tail_ps[:, j * 2 * EXPERTS:(j + 1) * 2 * EXPERTS], zs[c][:, j * P:(j + 1) * P],
                                       gate_split[:, :, :].rearrange("p h e -> p (h e)"), start=True, stop=True)
                    mm.then_inc(logits_ps_ready, 1)
                if step == GATES_TURN:
                    if c > 0:
                        reuse(pe, result_ready, n - 1)
                    lone_wait(pe, gates_ready, n + 1)
                    te.transpose(tail_ps[0:TILES * EXPERTS, 0:P], gates[:, :, :].rearrange("p t e -> p (t e)"),
                                 ident[:, :]).then_inc(gates_turned, 1)

            def project(m, c, q):
                n = CHUNKS * m + c
                pe.wait_ge(hid_done, EXPERTS * n + 2 * q + 2)
                reuse(pe, gated_done, EPAIRS * n + q)
                for a in range(2):
                    e = 2 * q + a
                    mm = te.matmul(y_ps[a * E:(a + 1) * E, :], w3_sb[:, e, :], hid[e % HIDS][:, :], start=True, stop=True)
                mm.then_inc(y_done, 1)

            def fold_sum(m, c, reader, count):
                pe.wait_ge(acc_done, (EPAIRS - 1) * (CHUNKS * m + c + 1))
                pe.wait_ge(reader, count)
                for j in range(TILES):
                    mm = te.matmul(tail_ps[:, j * E:(j + 1) * E], acc[c % 2][:, j * P:(j + 1) * P], fold[:, :],
                                   start=True, stop=True)
                mm.then_inc(folded, 1)

            def experts(m, k):
                c, e = divmod(k, EXPERTS)
                n, g = CHUNKS * m + c, SLOTS * m + k
                started = c > 0 or not isinstance(m, int) or m > 0
                if e == 0:
                    pe.wait_ge(z_split, split(m, c))
                    if isinstance(m, int) and m == 0 and c == 0:
                        pe.wait_ge(experts_ready, 2)
                        pe.wait_ge(experts_in, 16 * 5)
                for hi, lo, banks, reader, done in ((w1_hi, w1_lo, h1_ps, silu_done, h1_done),
                                                    (w2_hi, w2_lo, h2_ps, hid_done, h2_done)):
                    reuse(pe, reader, g - 1)
                    te.matmul(banks[k % 2][:, :], hi[:, e, :], zs[c][:, :], start=True, stop=False)
                    te.matmul(banks[k % 2][:, :], lo[:, e, :], zs[c][:, :], start=False, stop=True).then_inc(done, 1)
                if at := projected(m, k):
                    project(*at)
                if e == FOLD[c] and started:
                    if c < CHUNKS - 1:
                        fold_sum(*before(m, c), logits_ready, n + 2)
                    else:
                        fold_sum(*before(m, c), gatesT_ready, n + 1 if isinstance(m, int) and m == PAIRS - 1 else n + 2)
                for_routes(m, k, route)

            def attend_first(m, k):
                if isinstance(m, int) and m == 0 and k == QKV[0]:
                    setup_rest()
                attend(m, k)

            for_slots(pe, attend_first, experts)
            project(PAIRS - 1, CHUNKS - 1, EPAIRS - 1)
            fold_sum(PAIRS - 1, CHUNKS - 1, result_ready, CHUNKS * PAIRS - 1)


_INS = ["x", "L0_tok_W", "L0_tok_b", "L0_tok_pos_embed", "L0_attn_Wk", "L0_attn_bk", "L0_attn_Wq", "L0_attn_bq",
        "L0_attn_Wv", "L0_attn_bv", "L0_attn_Wr", "L0_attn_br", "L0_ffn_gate_w", "L0_ffn_gate_b",
        "L0_ffn_w1", "L0_ffn_w2", "L0_ffn_w3"]


def kernel(**inputs):
    import numpy as np
    import concourse.bacc as bacc
    from concourse.bass_utils import run_bass_kernel_spmd

    nc = bacc.Bacc("TRN2", target_bir_lowering=False, num_devices=1)
    arrays, args = {}, []
    for name in _INS:
        a = np.ascontiguousarray(inputs[name])
        arrays[f"in_{name}"] = a
        args.append(nc.dram_tensor(f"in_{name}", a.shape, mybir.dt.from_np(a.dtype), kind="ExternalInput").ap())
    out = nc.dram_tensor("out_0", (IMAGES, TOKENS, E), F32, kind="ExternalOutput").ap()
    vit_kernel(nc, *args, out)
    r = run_bass_kernel_spmd(nc, [arrays], core_ids=[0])
    return r.results[0]["out_0"]
```
